# Optimizing a Trainium2 kernel written in Bass

```python
import numpy as np
import jax
import jax.numpy as jnp

def _softmax(x, axis=-1):
    return jax.nn.softmax(x, axis=axis)

def _gelu(x):
    return jax.nn.gelu(x, approximate=True)

def _silu(x):
    return jax.nn.silu(x)

def _sigmoid(x):
    return jax.nn.sigmoid(x)

def _layernorm(x, axis=-1, eps=1e-05):
    m = jnp.mean(x, axis=axis, keepdims=True)
    v = jnp.var(x, axis=axis, keepdims=True)
    return (x - m) / jnp.sqrt(v + eps)

def _scatter_add(tgt, idx, src, axis=0):
    return tgt.at[idx].add(src)

def _segment_sum(src, seg, n):
    return jax.ops.segment_sum(src, seg, n)
kernel_name = 'mk_xattn_ffn_d1_seqx_r4_ed9e60'

def setup_inputs(seed: int=0):
    np.random.seed(seed)
    _w = jnp.asarray

    def _rec_inputs():
        import jax
        import jax.numpy as jnp
        _rk = jax.random.key(seed)
        x = 7.22e-05 + 1 * jax.random.normal(jax.random.fold_in(_rk, 1), (2, 1024, 256), jnp.float32)
        _lenS = 1024 - jax.random.randint(jax.random.fold_in(_rk, 7), (2,), 0, max(1, 1024 // 4) + 1, jnp.int32)
        _lenS2 = 154 - jax.random.randint(jax.random.fold_in(_rk, 8), (2,), 0, max(1, 154 // 4) + 1, jnp.int32)
        _ctx_1024P = jax.random.normal(jax.random.fold_in(_rk, 11), (2, 16, 256), jnp.float32)
        _ctx_1024c = jax.random.dirichlet(jax.random.fold_in(_rk, 511), 0.3 * jnp.ones((16,), jnp.float32), (2, 154))
        _ctx_1024t = jnp.einsum('bsk,bkd->bsd', _ctx_1024c, _ctx_1024P)
        _ctx_1024t = _ctx_1024t * jax.lax.rsqrt(jnp.mean(jnp.square(_ctx_1024t)) + 1e-12) * 0.953939
        ctx_1024 = 4.13588e-05 + 0.999923 * (_ctx_1024t + 0.3 * jax.random.normal(jax.random.fold_in(_rk, 611), (2, 154, 256), jnp.float32))
        return (x, ctx_1024)
    x, ctx_1024 = _rec_inputs()

    def _L0_xattn_setup():
        import jax, jax.numpy as jnp
        import numpy as np
        D_MODEL = 256
        NUM_HEADS = 16
        D_K = D_MODEL // NUM_HEADS
        key = jax.random.key(seed)
        ks = jax.random.split(key, 12)
        B, S = (4, 512)
        scale = 1.0 / np.sqrt(D_MODEL)
        inp = {'query': jax.random.normal(ks[0], (B, S, D_MODEL), jnp.float32), 'key': jax.random.normal(ks[1], (B, S, D_MODEL), jnp.float32), 'value': jax.random.normal(ks[2], (B, S, D_MODEL), jnp.float32), 'Wq': jax.random.normal(ks[3], (NUM_HEADS, D_MODEL, D_K), jnp.float32) * scale, 'bq': jax.random.normal(ks[4], (NUM_HEADS, D_K), jnp.float32) * 0.01, 'Wk': jax.random.normal(ks[5], (NUM_HEADS, D_MODEL, D_K), jnp.float32) * scale, 'bk': jax.random.normal(ks[6], (NUM_HEADS, D_K), jnp.float32) * 0.01, 'Wv': jax.random.normal(ks[7], (NUM_HEADS, D_MODEL, D_K), jnp.float32) * scale, 'bv': jax.random.normal(ks[8], (NUM_HEADS, D_K), jnp.float32) * 0.01, 'Wo': jax.random.normal(ks[9], (NUM_HEADS * D_K, D_MODEL), jnp.float32) * scale, 'bo': jax.random.normal(ks[10], (D_MODEL,), jnp.float32) * 0.01}
        return inp
    _L0_xattn_all = _L0_xattn_setup()
    _L0_xattn_in = {k: v for k, v in _L0_xattn_all.items() if k in ('Wq', 'bq', 'Wk', 'bk', 'Wv', 'bv', 'Wo', 'bo')}
    del _L0_xattn_all

    def _L0_ffn_setup():
        import jax, jax.numpy as jnp
        import numpy as np
        B, S, D, E, K = (4, 512, 256, 8, 2)
        H = 4 * D
        key = jax.random.key(seed)
        k0, k1, k2, k3 = jax.random.split(key, 4)
        x = jax.random.normal(k0, (B, S, D), dtype=jnp.float32)
        router_w = jax.random.normal(k1, (E, D), dtype=jnp.float32) * 0.02
        w1 = jax.random.normal(k2, (E, H, D), dtype=jnp.float32) * 0.02
        w2 = jax.random.normal(k3, (E, D, H), dtype=jnp.float32) * 0.02
        return {'x': x, 'router_w': router_w, 'w1': w1, 'w2': w2}
    _L0_ffn_all = _L0_ffn_setup()
    _L0_ffn_in = {k: v for k, v in _L0_ffn_all.items() if k in ('router_w', 'w1', 'w2')}
    del _L0_ffn_all
    return {'x': x, 'ctx_1024': ctx_1024, 'L0_xattn_Wq': _L0_xattn_in['Wq'], 'L0_xattn_bq': _L0_xattn_in['bq'], 'L0_xattn_Wk': _L0_xattn_in['Wk'], 'L0_xattn_bk': _L0_xattn_in['bk'], 'L0_xattn_Wv': _L0_xattn_in['Wv'], 'L0_xattn_bv': _L0_xattn_in['bv'], 'L0_xattn_Wo': _L0_xattn_in['Wo'], 'L0_xattn_bo': _L0_xattn_in['bo'], 'L0_ffn_router_w': _L0_ffn_in['router_w'], 'L0_ffn_w1': _L0_ffn_in['w1'], 'L0_ffn_w2': _L0_ffn_in['w2']}

def reference(x, ctx_1024, L0_xattn_Wq, L0_xattn_bq, L0_xattn_Wk, L0_xattn_bk, L0_xattn_Wv, L0_xattn_bv, L0_xattn_Wo, L0_xattn_bo, L0_ffn_router_w, L0_ffn_w1, L0_ffn_w2):
    import jax
    import jax.numpy as jnp

    def _L0_xattn_ref(query, key, value, Wq, bq, Wk, bk, Wv, bv, Wo, bo):
        import jax, jax.numpy as jnp
        import numpy as np
        D_MODEL = 256
        NUM_HEADS = 16
        D_K = D_MODEL // NUM_HEADS
        q = jnp.einsum('bsd,hdk->bhsk', query, Wq) + bq[None, :, None, :]
        k = jnp.einsum('bsd,hdk->bhsk', key, Wk) + bk[None, :, None, :]
        v = jnp.einsum('bsd,hdk->bhsk', value, Wv) + bv[None, :, None, :]
        scores = jnp.einsum('bhqk,bhsk->bhqs', q, k) / jnp.sqrt(jnp.asarray(D_K, q.dtype))
        attn = jax.nn.softmax(scores, axis=-1)
        heads = jnp.einsum('bhqs,bhsk->bhqk', attn, v)
        B, H, S, K = heads.shape
        concat = jnp.transpose(heads, (0, 2, 1, 3)).reshape(B, S, H * K)
        return concat @ Wo + bo

    def _L0_ffn_ref(x, router_w, w1, w2):
        import jax, jax.numpy as jnp
        import numpy as np
        B, S, D, E, K = (4, 512, 256, 8, 2)
        H = 4 * D
        b, s, d = x.shape
        e = router_w.shape[0]
        logits = jnp.einsum('bsd,ed->bse', x, router_w)
        probs = jax.nn.softmax(logits, axis=-1)
        topk_vals, topk_idx = jax.lax.top_k(probs, K)
        x_flat = x.reshape(b * s, d)
        vals = topk_vals.reshape(b * s, K)
        idx = topk_idx.reshape(b * s, K)
        out = jnp.zeros_like(x_flat)
        for eid in range(e):
            w = jnp.sum(jnp.where(idx == eid, vals, jnp.zeros((), x.dtype)), axis=-1)
            h = jax.nn.gelu(x_flat @ w1[eid].T, approximate=False)
            y = h @ w2[eid].T
            out = out + w[:, None] * y
        return out.reshape(b, s, d)
    x = x + _L0_xattn_ref(_layernorm(x, axis=-1), ctx_1024, ctx_1024, L0_xattn_Wq, L0_xattn_bq, L0_xattn_Wk, L0_xattn_bk, L0_xattn_Wv, L0_xattn_bv, L0_xattn_Wo, L0_xattn_bo)
    x = x + _L0_ffn_ref(_layernorm(x, axis=-1), L0_ffn_router_w, L0_ffn_w1, L0_ffn_w2)
    return x

_drawn_inputs = setup_inputs


def setup_inputs(seed=0):
    import zlib

    import numpy as np

    out = dict(_drawn_inputs(seed))
    spreads = {}
    factors = {'L0_xattn_bq': 29.946, 'L0_xattn_bk': 64.0, 'L0_xattn_bv': 6.735, 'L0_xattn_bo': 6.146}
    for name, (base, spread) in spreads.items():
        noise = np.random.default_rng([zlib.crc32(name.encode()), seed]).standard_normal(out[name].shape)
        drawn = base * np.exp(spread * noise) if base else spread * noise
        out[name] = jnp.asarray(drawn.astype(out[name].dtype))
    for name, factor in factors.items():
        out[name] = (out[name] * factor).astype(out[name].dtype)
    return out
```

```python
import numpy as np
import concourse.bass as bass
from concourse import mybir
from contextlib import ExitStack

B, S, D = 2, 1024, 256
KEYS = 154
HEADS, DK = 16, 16
E, HID = 8, 1024
TOK = B * S
P = 128
TILES = TOK // P
KC = D // P
REM = KEYS - P
GH = P // DK
GROUPS = HEADS // GH
QUADS = HEADS // 4
SLOTS = (2 * TOK + E * (P - 1)) // P
ROW = D + 4
HJ = HID // P
WB = KC * HID + HJ * D
VW = HEADS * 32 + QUADS * 64
EPS = 1e-5


def xattn_moe_kernel(nc, x, ctxT, wq, bq, wk, bk, wv, bv, wo, bo, rwT, wexp,
                     ident, headmask, before, em8, tokid, slots, out):
    fp32, f32r = mybir.dt.float32, mybir.dt.float32r
    bf16, i32 = mybir.dt.bfloat16, mybir.dt.int32
    ALU, ACT, AX = mybir.AluOpType, mybir.ActivationFunctionType, mybir.AxisListType

    routed = nc.dram_tensor("routed", [SLOTS * P, ROW], fp32).ap()

    with ExitStack() as ctx:
        def sb(name, shape, dt=fp32):
            return ctx.enter_context(nc.sbuf_tensor(name, shape, dt))

        def sem(name):
            return ctx.enter_context(nc.semaphore(name))

        id_sb = sb("id_sb", [P, P])
        mask_sb = sb("mask_sb", [P, GH])
        before_sb = sb("before_sb", [P, P])
        before_bf = sb("before_bf", [P, P], bf16)
        ones_bf = sb("ones_bf", [P, P], bf16)
        em8_sb = sb("em8_sb", [P, E])
        tokid_sb = sb("tokid_sb", [P, TILES + 1], i32)
        slots_sb = sb("slots_sb", [P, SLOTS])
        slotno_sb = sb("slotno_sb", [1, SLOTS])
        wq_sb = sb("wq_sb", [P, KC, D])
        wo_sb = sb("wo_sb", [P, KC, D])
        rw_sb = sb("rw_sb", [P, KC, E])
        bq_sb = sb("bq_sb", [P, GROUPS])
        bq4_sb = sb("bq4_sb", [P, GROUPS])
        bk_sb = sb("bk_sb", [P, GROUPS])
        bv_sb = sb("bv_sb", [P, D])
        bo_sb = sb("bo_sb", [P, D])
        half_sb = sb("half_sb", [P, 1])
        xs = sb("xs", [P, TILES, D])
        XR = sb("XR", [P, TILES, ROW])
        LG = sb("LG", [P, TILES, E])
        KBN = B * GROUPS * GH * KEYS
        KB = sb("KB", [P, 2 * KBN], f32r)
        kb_hi = KB[:, 0:KBN].rearrange("p (b g j k) -> p b g j k", b=B, g=GROUPS, j=GH)
        kb_lo = KB[:, KBN:2 * KBN].rearrange("p (b g j k) -> p b g j k", b=B, g=GROUPS, j=GH)
        V_all = sb("V_all", [P, B, VW])
        V_cur = sb("V_cur", [P, 2, VW])
        big = sb("big", [P, 2 * WB + 2048])
        DSZ = HEADS * KEYS
        diff = [big[:, u * DSZ:(u + 1) * DSZ].rearrange("p (h k) -> p h k", h=HEADS) for u in range(2)]
        o1 = 2 * DSZ
        pm = [big[:, o1 + u * HEADS * P:o1 + (u + 1) * HEADS * P].rearrange("p (h k) -> p h k", h=HEADS)
              for u in range(2)]
        o2 = o1 + 2 * HEADS * P
        ctx_sb = big[:, 0:KC * B * KEYS].rearrange("p (c n) -> p c n", c=KC)
        wk_sb = big[:, 1024:1024 + KC * D].rearrange("p (c n) -> p c n", c=KC)
        wv_sb = big[:, 2048:2048 + KC * D].rearrange("p (c n) -> p c n", c=KC)
        KT = big[:, 3072:3072 + GROUPS * B * KEYS].rearrange("p (g n) -> p g n", g=GROUPS)
        KTr = sb("KTr", [P, 2, GROUPS, B * KEYS], f32r)
        W = [big[:, u * WB:(u + 1) * WB] for u in range(2)]
        W1 = [w[:, 0:KC * HID].rearrange("p (c h) -> p c h", c=KC) for w in W]
        W2 = [w[:, KC * HID:WB].rearrange("p (j d) -> p j d", j=HJ) for w in W]
        pr = sb("pr", [P, 2, HEADS, 32])
        PT = sb("PT", [P, 5, 4, P])
        fold = sb("fold", [P, HEADS, 64])
        st1 = sb("st1", [P, 2, 6])
        mv1 = sb("mv1", [P, 2, 4])
        xn = sb("xn", [P, 2, D])
        xnT = sb("xnT", [P, 2, KC, P])
        qf = sb("qf", [P, 2, GROUPS, P])
        q_hi = sb("q_hi", [P, 2, GROUPS, P], f32r)
        q_lo = sb("q_lo", [P, 2, GROUPS, P], f32r)
        mx = sb("mx", [P, 2, 4])
        den = sb("den", [P, HEADS])
        rden = sb("rden", [P, HEADS, DK])
        rT = sb("rT", [P, GROUPS, P])
        OT = sb("OT", [P, 2, GROUPS, P])
        xb = sb("xb", [P, 2, D])
        x1 = sb("x1", [P, 2, D])
        st2 = sb("st2", [P, 2, 6])
        mv2 = sb("mv2", [P, 2, 4])
        xn2 = sb("xn2", [P, 2, D])
        xn2T = sb("xn2T", [P, KC, P])
        fill = sb("fill", [P, ROW])
        zero = sb("zero", [P, D])
        r_m1 = sb("r_m1", [P, TILES])
        r_m2 = sb("r_m2", [P, TILES])
        r_c = sb("r_c", [P, TILES])
        r_a = sb("r_a", [P, TILES, E])
        r_b = sb("r_b", [P, TILES, E])
        r_o1 = sb("r_o1", [P, TILES, E])
        r_o2 = sb("r_o2", [P, TILES, E])
        r_ex = sb("r_ex", [P, TILES, E])
        r_e2 = sb("r_e2", [P, TILES])
        r_s = sb("r_s", [P, TILES])
        r_pick = sb("r_pick", [P, TILES + 1, E], bf16)
        r_rank = sb("r_rank", [P, TILES + 1, E])
        r_i = sb("r_i", [P, E], i32)
        r_i2 = sb("r_i2", [P, E], i32)
        r_n = sb("r_n", [P, E])
        r_p = sb("r_p", [P, 2, 4 + E])
        r_st = sb("r_st", [P, E])
        r_base = sb("r_base", [P, E])
        r_pos = sb("r_pos", [P, 2, TILES])
        pos_i = sb("pos_i", [P, 2, TILES], i32)
        t_cmp = sb("t_cmp", [1, SLOTS, E])
        t_e = sb("t_e", [1, SLOTS])
        t_ei = sb("t_ei", [1, SLOTS], i32)
        t_par = sb("t_par", [1, SLOTS], i32)
        t_st = sb("t_st", [1, E], i32)
        XG = sb("XG", [P, 4, ROW])
        xgT = sb("xgT", [P, 2, KC, P])
        wrow = sb("wrow", [P, 4, 4])
        hid = sb("hid", [P, HID])
        hidT = sb("hidT", [P, HJ, P])
        ys = sb("ys", [P, 2, D])

        ps_s = [ctx.enter_context(nc.psum_tensor(f"ps_s{u}", [P, 2, 512], fp32)) for u in range(2)]
        ps_t = [ctx.enter_context(nc.psum_tensor(f"ps_t{u}", [P, 512], fp32)) for u in range(2)]
        ps_a = ctx.enter_context(nc.psum_tensor("ps_a", [P, 512], fp32))
        ps_c = ctx.enter_context(nc.psum_tensor("ps_c", [P, 512], fp32))

        ld_ctx, ld_w, ld_c, ld_x0, ld_x1 = (sem(n) for n in ("ld_ctx", "ld_w", "ld_c", "ld_x0", "ld_x1"))
        fill_made, fill_stored = sem("fill_made"), sem("fill_stored")
        const_made, v_zeroed, p_zeroed = sem("const_made"), sem("v_zeroed"), sem("p_zeroed")
        bq_made = sem("bq_made")
        k_psum, k_made, kt_hi, kt_lo, kb_made = (sem(n) for n in ("k_psum", "k_made", "kt_hi", "kt_lo", "kb_made"))
        v_psum, v_made = sem("v_psum"), sem("v_made")
        st1_made, mv1_made, var1_made, rstd1_made = (sem(n) for n in ("st1_made", "mv1_made", "var1_made", "rstd1_made"))
        xn_made, xnT_psum, xnT_made = sem("xn_made"), sem("xnT_psum"), sem("xnT_made")
        q_psum, qf_made, q_hi_made, q_split = sem("q_psum"), sem("qf_made"), sem("q_hi_made"), sem("q_split")
        s_psum, mx_made, diff_made, p_made, pr_made = (sem(n) for n in ("s_psum", "mx_made", "diff_made", "p_made", "pr_made"))
        t_psum, t_made = sem("t_psum"), sem("t_made")
        fold1, fold_made, den_made, rden_made = sem("fold1"), sem("fold_made"), sem("den_made"), sem("rden_made")
        vcur_made, pv_psum, rT_psum, rT_made, OT_made = (sem(n) for n in ("vcur_made", "pv_psum", "rT_psum", "rT_made", "OT_made"))
        xb_made, wo_psum, x1_made = sem("xb_made"), sem("wo_psum"), sem("x1_made")
        x1_stored = [sem(f"x1_stored{u}") for u in range(2)]
        xr_stored = [sem(f"xr_stored{u}") for u in range(2)]
        st2_made, mv2_made, var2_made, rstd2_made, xn2_made = (sem(n) for n in ("st2_made", "mv2_made", "var2_made", "rstd2_made", "xn2_made"))
        xn2T_psum, xn2T_made, lg_psum, lg_made = (sem(n) for n in ("xn2T_psum", "xn2T_made", "lg_psum", "lg_made"))
        r_step, r_shift, r_exp, pick_made, rank_psum = (sem(n) for n in ("r_step", "r_shift", "r_exp", "pick_made", "rank_psum"))
        rows_made, tables_made, scattered = sem("rows_made"), sem("tables_made"), sem("scattered")
        w_loaded = sem("w_loaded")
        xg_loaded = [sem(f"xg_loaded{u}") for u in range(4)]
        xgT_psum, xgT_made, wr1, wr2, wr3, wrow_made = (sem(n) for n in ("xgT_psum", "xgT_made", "wr1", "wr2", "wr3", "wrow_made"))
        up_psum, hid_made, hidT_psum, hidT_made_a, hidT_made_v = (sem(n) for n in ("up_psum", "hid_made", "hidT_psum", "hidT_made_a", "hidT_made_v"))
        down_psum, ys_made, added = sem("down_psum"), sem("ys_made"), sem("added")

        dve_passed, pool_passed = sem("dve_passed"), sem("pool_passed")

        block = ctx.enter_context(nc.Block())

        LOOP0, LOOP1 = 4, TILES - 2

        def steps(eng, step):
            for t in range(LOOP0):
                step(t, t % 2, t // 2, lambda d, t=t: 0 <= t + d < TILES)
            with eng.Fori(LOOP0 // 2, LOOP1 // 2) as i:
                for u in range(2):
                    step(2 * i + u, u, i, lambda d: True)
            for t in range(LOOP1, TILES + 2):
                step(t, t % 2, t // 2, lambda d, t=t: 0 <= t + d < TILES)

        FF_LOOP = (SLOTS - 3) // 4 * 4

        def ff_slots(eng, slot):
            for s in range(4):
                slot(s, s, 0, lambda d: True)
            with eng.Fori(1, FF_LOOP // 4) as i:
                for u in range(4):
                    slot(4 * i + u, u, i, lambda d: True)
            for s in range(FF_LOOP, SLOTS):
                slot(s, s % 4, s // 4, lambda d, s=s: s + d < SLOTS)

        @block.sync
        def _(sp):
            sp.dma_start(ctx_sb, ctxT.rearrange("(c p) n -> p c n", p=P)).then_inc(ld_ctx, 16)
            sp.dma_start(wk_sb, wk.rearrange("(c p) n -> p c n", p=P)).then_inc(ld_ctx, 16)
            sp.dma_start(wv_sb, wv.rearrange("(c p) n -> p c n", p=P)).then_inc(ld_ctx, 16)
            sp.dma_start(bk_sb[:, :], bk.rearrange("(g p) -> p g", p=P),
                         allow_slow_non_contiguous=True).then_inc(ld_ctx, 16)
            sp.dma_start(bv_sb[:, :], bv.unsqueeze(0).to_broadcast([P, D])).then_inc(ld_ctx, 16)
            sp.dma_start(mask_sb[:, :], headmask).then_inc(ld_ctx, 16)
            sp.dma_start(before_sb[:, :], before).then_inc(ld_c, 16)
            sp.dma_start(em8_sb[:, :], em8).then_inc(ld_c, 16)
            sp.dma_start(tokid_sb[:, :], tokid).then_inc(ld_c, 16)
            sp.dma_start(slots_sb[:, :], slots[0:P, :]).then_inc(ld_c, 16)
            sp.dma_start(slotno_sb[:, :], slots[P:P + 1, :]).then_inc(ld_c, 16)
            sp.wait_ge(fill_made, 3)
            sp.dma_start(routed.rearrange("(s p) c -> p s c", p=P),
                         fill[:, :].unsqueeze(1).to_broadcast([P, SLOTS, ROW])).then_inc(fill_stored, 16)
            sp.dma_start(out[TOK:TOK + P, :], zero[:, :]).then_inc(fill_stored, 16)

            def step(t, u, i, has):
                if has(-2):
                    sp.wait_ge(x1_made, t - 1)
                    sp.dma_start(out[bass.ds((t - 2) * P, P), :], x1[:, u, :]).then_inc(x1_stored[u], 16)
                    sp.wait_ge(xn2_made, t - 1)
                    sp.dma_start(XR[:, bass.ds(t - 2, 1), 0:D], xn2[:, u:u + 1, :]).then_inc(xr_stored[u], 16)
            steps(sp, step)

            sp.wait_ge(t_psum, 5 * TILES)
            sp.wait_ge(fold_made, TILES)
            sp.dma_start(W[0], wexp[0]).then_inc(w_loaded, 16)
            sp.wait_ge(w_loaded, 16)
            sp.dma_start(W[1], wexp[1]).then_inc(w_loaded, 16)
            sp.wait_ge(tables_made, 1)
            for e in range(2, E):
                start = sp.value_load(t_st[0:1, e - 1:e], min_val=1, max_val=SLOTS)
                sp.wait_ge(down_psum, start)
                sp.wait_ge(w_loaded, 16 * e)
                sp.dma_start(W[e % 2], wexp[e]).then_inc(w_loaded, 16)
            sp.wait_ge(added, 16 * SLOTS)

        @block.gpsimd
        def _(pool):
            pool.memset(half_sb[:, :], -0.5).then_inc(const_made, 1)
            pool.memset(fill[:, :], 0.0).then_inc(fill_made, 1)
            pool.memset(zero[:, :], 0.0)
            pool.memset(V_all[:, :, :], 0.0).then_inc(v_zeroed, 1)
            pool.memset(pr[:, :, :, :], 0.0).then_inc(p_zeroed, 1)
            pool.memset(ones_bf[:, :], 1.0).then_inc(const_made, 1)
            pool.wait_ge(ld_c, 80)
            pool.wait_ge(fill_made, 1)
            pool.tensor_copy(fill[:, D:D + 1].bitcast(i32), tokid_sb[:, TILES:TILES + 1]).then_inc(fill_made, 1)
            pool.memset(fill[:, ROW - 1:ROW], -1.0).then_inc(fill_made, 1)
            pool.tensor_copy(XR[:, :, D].bitcast(i32), tokid_sb[:, 0:TILES]).then_inc(const_made, 1)
            pool.wait_ge(const_made, 3)

            def wait_alone(s, n):
                pool.wait_ge(s, n)
                if not isinstance(n, int):
                    pool.sem_inc(pool_passed, 1)

            def rstd(t, u, stats, made, rstd_made):
                pool.wait_ge(made, t + 1)
                pool.tensor_tensor(stats[:, u, 3:4], stats[:, u, 2:3], half_sb[:, :], ALU.pow).then_inc(rstd_made, 1)

            def xs_tile(t):
                return xs[:, bass.ds(t, 1), :].squeeze(1) if not isinstance(t, int) else xs[:, t, :]

            def split_q(t, u):
                pool.wait_ge(qf_made, t + 1)
                if not isinstance(t, int) or t >= 2:
                    wait_alone(s_psum, 4 * (t - 1))
                pool.tensor_copy(q_hi[:, u, :, :], qf[:, u, :, :]).then_inc(q_hi_made, 1)
                pool.wait_ge(q_hi_made, t + 1)
                pool.tensor_tensor(q_lo[:, u, :, :], qf[:, u, :, :], q_hi[:, u, :, :].bitcast(fp32),
                                   ALU.subtract).then_inc(q_split, 1)

            rstd(0, 0, mv1, var1_made, rstd1_made)
            rstd(1, 1, mv1, var1_made, rstd1_made)
            split_q(0, 0)
            pool.wait_ge(v_made, B * 6)

            def step(t, u, i, has):
                v = 1 - u
                if has(-1):
                    pool.wait_ge(p_made, 4 * t)
                    pool.wait_ge(pr_made, t)
                    if not isinstance(t, int) or t >= 2:
                        pool.wait_ge(den_made, t - 1)
                    pool.tensor_tensor(fold[:, :, :], pm[v][:, :, 0:64], pm[v][:, :, 64:128], ALU.add).then_inc(fold1, 1)
                    pool.wait_ge(fold1, t)
                    pool.tensor_tensor(fold[:, :, 0:32], fold[:, :, 0:32], pr[:, v, :, :], ALU.add).then_inc(fold_made, 1)
                if has(-2):
                    rstd(t - 2, u, mv2, var2_made, rstd2_made)
                if has(1):
                    split_q(t + 1, v)
                if has(2):
                    rstd(t + 2, u, mv1, var1_made, rstd1_made)
                if has(-1):
                    if not isinstance(t, int) or t >= 3:
                        pool.wait_ge(x1_made, t - 2)
                    pool.tensor_tensor(xb[:, v, :], xs_tile(t - 1), bo_sb[:, :], ALU.add).then_inc(xb_made, 1)
                if has(0):
                    if not isinstance(t, int) or t >= 2:
                        wait_alone(pv_psum, t - 1)
                    if isinstance(t, int):
                        src = V_all[:, t // (TILES // B), :]
                    else:
                        src = V_all[:, bass.ds(t // (TILES // B), 1), :].squeeze(1)
                    pool.tensor_copy(V_cur[:, u, :], src).then_inc(vcur_made, 1)

            pool.wait_ge(ld_w, 16 * 6)
            steps(pool, step)

            pool.wait_ge(rows_made, 1)
            pool.wait_ge(fill_stored, 32)
            for u in range(2):
                pool.wait_ge(xr_stored[u], 16 * TILES // 2)
            for t in range(TILES):
                for k in range(2):
                    pool.indirect_dma_start(routed, bass.IndirectOffsetOnAxis(pos_i[:, k, t:t + 1], 0),
                                            XR[:, t, :], None).then_inc(scattered, 16)
            pool.wait_ge(scattered, 16 * 2 * TILES)
            for u in range(2):
                pool.wait_ge(x1_stored[u], 16 * TILES // 2)

            def load_rows(s, u):
                pool.dma_start(XG[:, u, :], routed[bass.ds(s * P, P), :]).then_inc(xg_loaded[u], 16)

            for s in range(3):
                load_rows(s, s)

            def slot(s, u, i, has):
                wait_alone(ys_made, s + 1)
                if not isinstance(s, int) or s >= 1:
                    wait_alone(added, 16 * s)
                pool.indirect_dma_start(out, bass.IndirectOffsetOnAxis(XG[:, u, D:D + 1].bitcast(i32), 0),
                                        ys[:, u % 2, :], None, compute_op=ALU.add).then_inc(added, 16)
                if has(3):
                    load_rows(s + 3, (u + 3) % 4)
            ff_slots(pool, slot)

        @block.scalar
        def _(act):
            def to_cols(v, ap):
                return act.dma_start(ap, v.rearrange("(g p) -> p g", p=P), allow_slow_non_contiguous=True)
            xv = x.rearrange("(t p) d -> p t d", p=P)
            act.dma_start(xs[:, 0:4, :], xv[:, 0:4, :]).then_inc(ld_x0, 16)
            act.dma_start(id_sb[:, :], ident).then_inc(ld_w, 16)
            act.dma_start(wq_sb[:, :, :], wq.rearrange("(c p) n -> p c n", p=P)).then_inc(ld_w, 16)
            to_cols(bq, bq_sb[:, :]).then_inc(ld_w, 16)
            act.dma_start(xs[:, 4:TILES, :], xv[:, 4:TILES, :]).then_inc(ld_x1, 16)
            act.dma_start(wo_sb[:, :, :], wo.rearrange("(c p) n -> p c n", p=P)).then_inc(ld_w, 16)
            act.dma_start(rw_sb[:, :, :], rwT.rearrange("(c p) n -> p c n", p=P)).then_inc(ld_w, 16)
            act.dma_start(bo_sb[:, :], bo.unsqueeze(0).to_broadcast([P, D])).then_inc(ld_w, 16)
            act.wait_ge(ld_w, 96)
            act.mul(bq4_sb[:, :], bq_sb[:, :], DK ** -0.5).then_inc(bq_made, 1)
            act.wait_ge(bq_made, 1)

            def evac_xnT(t, u):
                act.wait_ge(xnT_psum, t + 1)
                if not isinstance(t, int) or t >= 2:
                    act.wait_ge(q_psum, t - 1)
                act.activation(xnT[:, u, :, :], ps_a[:, 0:KC * P].rearrange("p (c n) -> p c n", c=KC),
                               ACT.Copy).then_inc(xnT_made, 1)

            def evac_q(t, u):
                act.wait_ge(q_psum, t + 1)
                if not isinstance(t, int) or t >= 2:
                    act.wait_ge(q_split, t - 1)
                for g in range(GROUPS):
                    last = act.activation(qf[:, u, g, :], ps_a[:, D + g * P:D + (g + 1) * P], ACT.Identity,
                                          bias=bq4_sb[:, g:g + 1], scale=DK ** -0.5)
                last.then_inc(qf_made, 1)

            evac_xnT(0, 0)
            evac_q(0, 0)
            act.wait_ge(p_zeroed, 1)
            act.wait_ge(kb_made, B * GROUPS * 2)

            def exp(t, u, q):
                act.wait_ge(diff_made, 4 * t + q + 1)
                if q == 0 and (not isinstance(t, int) or t >= 2):
                    act.wait_ge(fold_made, t - 1)
                    act.wait_ge(t_psum, 5 * (t - 1))
                act.activation(pm[u][:, 4 * q:4 * q + 4, :], diff[u][:, 4 * q:4 * q + 4, 0:P],
                               ACT.Exp).then_inc(p_made, 1)

            def evac_t(t, k, u):
                act.wait_ge(t_psum, 5 * t + k + 1)
                if not isinstance(t, int) or t >= 1:
                    act.wait_ge(pv_psum, t)
                act.activation(PT[:, k, :, :], ps_t[(5 * u + k) % 2][:, :].rearrange("p (a n) -> p a n", a=4),
                               ACT.Copy).then_inc(t_made, 1)

            def step(t, u, i, has):
                v = 1 - u
                if has(0):
                    exp(t, u, 0)
                if has(1):
                    evac_xnT(t + 1, v)
                if has(-1):
                    evac_t(t - 1, 2, v)
                if has(0):
                    exp(t, u, 1)
                if has(1):
                    evac_q(t + 1, v)
                if has(-1):
                    evac_t(t - 1, 3, v)
                    evac_t(t - 1, 4, v)
                if has(0):
                    exp(t, u, 2)
                if has(-2):
                    act.wait_ge(xn2T_psum, t - 1)
                    if not isinstance(t, int) or t >= 3:
                        act.wait_ge(lg_psum, t - 2)
                    act.activation(xn2T[:, :, :], ps_c[:, 0:KC * P].rearrange("p (c n) -> p c n", c=KC),
                                   ACT.Copy).then_inc(xn2T_made, 1)
                if has(-1):
                    act.wait_ge(rT_psum, t)
                    if not isinstance(t, int) or t >= 2:
                        act.wait_ge(OT_made, t - 1)
                    act.activation(rT[:, :, :], ps_a[:, D:2 * D].rearrange("p (g n) -> p g n", g=GROUPS),
                                   ACT.Copy).then_inc(rT_made, 1)
                if has(0):
                    evac_t(t, 0, u)
                    exp(t, u, 3)
                    act.activation(pr[:, u, :, 0:REM], diff[u][:, :, P:KEYS], ACT.Exp).then_inc(pr_made, 1)
                    evac_t(t, 1, u)
            steps(act, step)

            act.wait_ge(r_shift, 1)
            act.activation(r_ex[:, :, :], r_a[:, :, :], ACT.Exp).then_inc(r_exp, 1)
            act.wait_ge(r_shift, 2)
            act.activation(r_e2[:, :], r_s[:, :], ACT.Exp).then_inc(r_exp, 1)

            def gelu(s):
                act.wait_ge(up_psum, s + 1)
                if not isinstance(s, int) or s >= 1:
                    act.wait_ge(hidT_psum, s)
                act.activation(hid[:, :].rearrange("p (c n) -> p c n", c=2), ps_s[0][:, :, :],
                               ACT.Gelu).then_inc(hid_made, 1)
            gelu(0)

            def slot(s, u, i, has):
                act.wait_ge(hidT_psum, s + 1)
                if not isinstance(s, int) or s >= 1:
                    act.wait_ge(down_psum, s)
                act.activation(hidT[:, 4:8, :], ps_t[1][:, :].rearrange("p (a n) -> p a n", a=4),
                               ACT.Copy).then_inc(hidT_made_a, 1)
                if has(1):
                    gelu(s + 1)
            ff_slots(act, slot)

        @block.vector
        def _(dve):
            dve.wait_ge(ld_x0, 16)

            def wait_alone(s, n):
                dve.wait_ge(s, n)
                if not isinstance(n, int):
                    dve.sem_inc(dve_passed, 1)

            def stats1(t, u):
                if not isinstance(t, int) or t >= 2:
                    dve.wait_ge(xn_made, t - 1)
                xt = xs[:, t, :] if isinstance(t, int) else xs[:, bass.ds(t, 1), :].squeeze(1)
                dve.bn_stats(st1[:, u, :], xt).then_inc(st1_made, 1)
                aggregate(t, u, st1, st1_made, mv1, mv1_made, var1_made)

            def aggregate(t, u, st, st_made, mv, mv_made, var_made):
                wait_alone(st_made, t + 1)
                dve.bn_aggr(mv[:, u, 0:2], st[:, u, :]).then_inc(mv_made, 1)
                dve.wait_ge(mv_made, t + 1)
                dve.tensor_scalar(mv[:, u, 2:3], mv[:, u, 1:2], EPS, None, ALU.add).then_inc(var_made, 1)

            def norm1(t, u):
                dve.wait_ge(rstd1_made, t + 1)
                if not isinstance(t, int) or t >= 2:
                    dve.wait_ge(xnT_psum, t - 1)
                xt = xs[:, t, :] if isinstance(t, int) else xs[:, bass.ds(t, 1), :].squeeze(1)
                dve.tensor_scalar(xn[:, u, :], xt, mv1[:, u, 0:1], mv1[:, u, 3:4],
                                  ALU.subtract, ALU.mult).then_inc(xn_made, 1)

            def norm2(t, u, i):
                dve.wait_ge(rstd2_made, t + 1)
                if not isinstance(t, int) or t >= 2:
                    dve.wait_ge(xr_stored[u], 16 * i)
                    dve.wait_ge(xn2T_psum, t - 1)
                dve.tensor_scalar(xn2[:, u, :], x1[:, u, :], mv2[:, u, 0:1], mv2[:, u, 3:4],
                                  ALU.subtract, ALU.mult).then_inc(xn2_made, 1)
            stats1(0, 0)
            stats1(1, 1)
            norm1(0, 0)
            norm1(1, 1)

            dve.wait_ge(ld_ctx, 96)
            dve.wait_ge(k_psum, 1)
            for g in range(GROUPS):
                dve.tensor_scalar(KT[:, g, :], ps_s[0][:, g, 0:B * KEYS], bk_sb[:, g:g + 1], None,
                                  ALU.add).then_inc(k_made, 1)
            dve.wait_ge(k_made, 2)
            dve.tensor_copy(KTr[:, 0, :, :], KT).then_inc(kt_hi, 1)
            dve.wait_ge(kt_hi, 1)
            dve.tensor_tensor(KTr[:, 1, :, :], KT, KTr[:, 0, :, :].bitcast(fp32), ALU.subtract).then_inc(kt_lo, 1)
            dve.wait_ge(kt_lo, 1)
            for b in range(B):
                for g in range(GROUPS):
                    for part, kb in ((0, kb_hi), (1, kb_lo)):
                        src = KTr[:, part, g, b * KEYS:(b + 1) * KEYS].bitcast(fp32)
                        dve.tensor_tensor(kb[:, b, g, :, :], src.unsqueeze(1).to_broadcast([P, GH, KEYS]),
                                          mask_sb[:, :].unsqueeze(2).to_broadcast([P, GH, KEYS]),
                                          ALU.mult).then_inc(kb_made, 1)
            dve.wait_ge(v_psum, 1)
            dve.wait_ge(v_zeroed, 1)
            for b in range(B):
                vm = V_all[:, b, 0:HEADS * 32].rearrange("p (r a c) -> p r a c", a=2, c=32)
                vr = V_all[:, b, HEADS * 32:VW].rearrange("p (q c) -> p q c", c=64)
                main = ps_s[1][:, b, 0:D].rearrange("p (r a c) -> p r a c", a=2, c=DK)
                bvm = bv_sb[:, :].rearrange("p (r a c) -> p r a c", a=2, c=DK)
                for a in range(2):
                    dve.tensor_tensor(vm[:, :, a, DK * a:DK * a + DK], main[:, :, a, :], bvm[:, :, a, :],
                                      ALU.add).then_inc(v_made, 1)
                for j in range(4):
                    lanes = slice(32 * j, 32 * j + REM)
                    rest = ps_s[1][lanes, b, D:2 * D].rearrange("p (q j c) -> p q j c", j=4, c=DK)
                    bvr = bv_sb[lanes, :].rearrange("p (q j c) -> p q j c", j=4, c=DK)
                    dve.tensor_tensor(vr[lanes, :, DK * j:DK * j + DK], rest[:, :, j, :], bvr[:, :, j, :],
                                      ALU.add).then_inc(v_made, 1)

            dve.wait_ge(ld_x1, 16)
            dve.wait_ge(kb_made, B * GROUPS * 2)

            def scores(t, u, q):
                n = 4 * t + q
                dve.wait_ge(s_psum, n + 1)
                src = ps_s[q % 2][:, :, 0:2 * KEYS].rearrange("p b (h k) -> p b h k", h=2)
                m = mx[:, q % 2, :].rearrange("p (b h) -> p b h", b=2)
                dve.tensor_reduce(m, src, AX.X, ALU.max).then_inc(mx_made, 1)
                dve.wait_ge(mx_made, n + 1)
                if q == 0 and (not isinstance(t, int) or t >= 2):
                    dve.wait_ge(pr_made, t - 1)
                dst = diff[u][:, 4 * q:4 * q + 4, :].rearrange("p (b h) k -> p b h k", b=2)
                dve.tensor_tensor(dst, src, m.unsqueeze(3).to_broadcast([P, 2, 2, KEYS]),
                                  ALU.subtract).then_inc(diff_made, 1)

            def step(t, u, i, has):
                v = 1 - u
                if has(0):
                    scores(t, u, 0)
                if has(-2):
                    dve.wait_ge(wo_psum, t - 1)
                    dve.wait_ge(xb_made, t - 1)
                    if not isinstance(t, int) or t >= 4:
                        dve.wait_ge(x1_stored[u], 16 * (i - 1))
                        dve.wait_ge(xn2_made, t - 3)
                    dve.tensor_tensor(x1[:, u, :], ps_c[:, 0:D], xb[:, u, :], ALU.add).then_inc(x1_made, 1)
                    dve.wait_ge(x1_made, t - 1)
                    dve.bn_stats(st2[:, u, :], x1[:, u, :]).then_inc(st2_made, 1)
                    aggregate(t - 2, u, st2, st2_made, mv2, mv2_made, var2_made)
                if has(0):
                    scores(t, u, 1)
                if has(-2):
                    norm2(t - 2, u, i - 1)
                if has(2):
                    stats1(t + 2, u)
                if has(-1):
                    dve.wait_ge(fold_made, t)
                    dve.tensor_reduce(den[:, :], fold[:, :, :], AX.X, ALU.add).then_inc(den_made, 1)
                    dve.wait_ge(den_made, t)
                    if not isinstance(t, int) or t >= 2:
                        dve.wait_ge(rT_psum, t - 1)
                    dve.reciprocal(rden[:, :, :], den[:, :].unsqueeze(2).to_broadcast([P, HEADS, DK]))\
                       .then_inc(rden_made, 1)
                if has(0):
                    scores(t, u, 2)
                if has(2):
                    norm1(t + 2, u)
                if has(0):
                    scores(t, u, 3)
                if has(-1):
                    dve.wait_ge(rT_made, t)
                    if not isinstance(t, int) or t >= 3:
                        dve.wait_ge(wo_psum, t - 2)
                    dve.tensor_tensor(OT[:, v, :, :], ps_a[:, 0:D].rearrange("p (g n) -> p g n", g=GROUPS),
                                      rT[:, :, :], ALU.mult).then_inc(OT_made, 1)
                if has(-2):
                    dve.wait_ge(lg_psum, t - 1)
                    lt = LG[:, t - 2, :] if isinstance(t, int) else LG[:, bass.ds(t - 2, 1), :].squeeze(1)
                    dve.tensor_copy(lt, ps_c[:, 0:E]).then_inc(lg_made, 1)
            steps(dve, step)

            done = [0]

            def then(ins):
                done[0] += 1
                ins.then_inc(r_step, 1)
                dve.wait_ge(r_step, done[0])

            wide = [P, TILES, E]
            bc_t = lambda a: a.unsqueeze(2).to_broadcast(wide)
            bc_e = lambda a: a.unsqueeze(1).to_broadcast(wide)
            dve.wait_ge(lg_made, TILES)
            dve.wait_ge(ld_c, 80)
            then(dve.tensor_copy(before_bf[:, :], before_sb[:, :]))

            def top(src, m, o):
                then(dve.tensor_reduce(m, src, AX.X, ALU.max))
                then(dve.tensor_tensor(r_b[:, :, :], src, bc_t(m), ALU.is_ge))
                then(dve.tensor_tensor(r_b[:, :, :], r_b[:, :, :], bc_e(em8_sb[:, :]), ALU.mult))
                then(dve.tensor_reduce(r_c[:, :], r_b[:, :, :], AX.X, ALU.min))
                then(dve.tensor_tensor(o, bc_e(em8_sb[:, :]), bc_t(r_c[:, :]), ALU.is_equal))

            top(LG[:, :, :], r_m1[:, :], r_o1[:, :, :])
            dve.tensor_tensor(r_a[:, :, :], LG[:, :, :], bc_t(r_m1[:, :]), ALU.subtract).then_inc(r_shift, 1)
            then(dve.scalar_tensor_tensor(r_rank[:, 0:TILES, :], r_o1[:, :, :], -3e38, LG[:, :, :], ALU.mult, ALU.add))
            top(r_rank[:, 0:TILES, :], r_m2[:, :], r_o2[:, :, :])
            dve.tensor_tensor(r_s[:, :], r_m2[:, :], r_m1[:, :], ALU.subtract).then_inc(r_shift, 1)
            then(dve.memset(r_pick[:, TILES, :], 0.0))
            dve.tensor_tensor(r_pick[:, 0:TILES, :], r_o1[:, :, :], r_o2[:, :, :], ALU.add).then_inc(pick_made, 1)
            dve.wait_ge(r_exp, 2)
            then(dve.tensor_reduce(r_c[:, :], r_ex[:, :, :], AX.X, ALU.add))
            then(dve.reciprocal(XR[:, :, D + 1], r_c[:, :]))
            then(dve.tensor_tensor(XR[:, :, D + 2], r_e2[:, :], XR[:, :, D + 1], ALU.mult))
            dve.wait_ge(rank_psum, 1)
            then(dve.tensor_copy(r_rank[:, :, :], ps_a[:, 0:(TILES + 1) * E].rearrange("p (t e) -> p t e", e=E)))
            then(dve.tensor_scalar(r_i[:, :], r_rank[:, TILES, :], float(P - 1), None, ALU.add))
            then(dve.tensor_scalar(r_i2[:, :], r_i[:, :], 7, None, ALU.logical_shift_right))
            then(dve.tensor_scalar(r_n[:, :], r_i2[:, :], 1.0, None, ALU.max))
            then(dve.memset(r_p[:, :, :], 0.0))
            then(dve.tensor_copy(r_p[:, 0, 4:4 + E], r_n[:, :]))
            for n, d in enumerate((1, 2, 4)):
                then(dve.tensor_tensor(r_p[:, 1 - n % 2, 4:4 + E], r_p[:, n % 2, 4:4 + E],
                                       r_p[:, n % 2, 4 - d:4 + E - d], ALU.add))
            then(dve.tensor_tensor(r_st[:, :], r_p[:, 1, 4:4 + E], r_n[:, :], ALU.subtract))
            then(dve.tensor_scalar(r_base[:, :], r_st[:, :], float(P), None, ALU.mult))
            then(dve.tensor_tensor(r_a[:, :, :], r_rank[:, 0:TILES, :], bc_e(r_base[:, :]), ALU.add))
            for k, o in ((0, r_o1), (1, r_o2)):
                then(dve.tensor_tensor(r_b[:, :, :], r_a[:, :, :], o[:, :, :], ALU.mult))
                then(dve.tensor_reduce(r_pos[:, k, :], r_b[:, :, :], AX.X, ALU.add))
            then(dve.tensor_copy(XR[:, :, D + 3], r_pos[:, 0, :]))
            dve.tensor_copy(pos_i[:, :, :], r_pos[:, :, :]).then_inc(rows_made, 1)
            then(dve.tensor_tensor(t_cmp[:, :, :], slotno_sb[:, :].unsqueeze(2).to_broadcast([1, SLOTS, E]),
                                   r_st[0:1, :].unsqueeze(1).to_broadcast([1, SLOTS, E]), ALU.is_ge))
            then(dve.tensor_reduce(t_e[:, :], t_cmp[:, :, :], AX.X, ALU.add))
            then(dve.tensor_scalar(t_ei[:, :], t_e[:, :], -1.0, None, ALU.add))
            then(dve.tensor_scalar(t_par[:, :], t_ei[:, :], 1, None, ALU.bitwise_and))
            dve.tensor_copy(t_st[:, :], r_st[0:1, :]).then_inc(tables_made, 1)

            def take_rows(s, u):
                dve.wait_ge(xgT_psum, s + 1)
                if not isinstance(s, int) or s >= 2:
                    dve.wait_ge(up_psum, s - 1)
                dve.tensor_copy(xgT[:, u % 2, :, :], ps_c[:, 0:D].rearrange("p (c n) -> p c n", c=KC))\
                   .then_inc(xgT_made, 1)
                sl = slots_sb[:, s:s + 1] if isinstance(s, int) else slots_sb[:, bass.ds(s, 1)]
                dve.tensor_tensor(wrow[:, u, 0:1], XG[:, u, D + 3:D + 4], sl, ALU.is_equal).then_inc(wr1, 1)
                dve.wait_ge(wr1, s + 1)
                dve.tensor_scalar(wrow[:, u, 1:2], wrow[:, u, 0:1], -1.0, 1.0, ALU.mult, ALU.add).then_inc(wr2, 1)
                dve.wait_ge(wr2, s + 1)
                dve.tensor_tensor(wrow[:, u, 2:3], wrow[:, u, 1:2], XG[:, u, D + 2:D + 3], ALU.mult).then_inc(wr3, 1)
                dve.wait_ge(wr3, s + 1)
                dve.scalar_tensor_tensor(wrow[:, u, 3:4], wrow[:, u, 0:1], XG[:, u, D + 1:D + 2], wrow[:, u, 2:3],
                                         ALU.mult, ALU.add).then_inc(wrow_made, 1)
            take_rows(0, 0)
            take_rows(1, 1)

            def slot(s, u, i, has):
                dve.wait_ge(hidT_psum, s + 1)
                if not isinstance(s, int) or s >= 1:
                    dve.wait_ge(down_psum, s)
                dve.tensor_copy(hidT[:, 0:4, :], ps_t[0][:, :].rearrange("p (a n) -> p a n", a=4))\
                   .then_inc(hidT_made_v, 1)
                if has(2):
                    take_rows(s + 2, (u + 2) % 4)
                dve.wait_ge(down_psum, s + 1)
                dve.wait_ge(wrow_made, s + 1)
                if not isinstance(s, int) or s >= 2:
                    dve.wait_ge(added, 16 * (s - 1))
                dve.tensor_scalar(ys[:, u % 2, :], ps_s[1][:, u % 2, 0:D], wrow[:, u, 3:4], None,
                                  ALU.mult).then_inc(ys_made, 1)
            ff_slots(dve, slot)

        @block.tensor
        def _(pe):
            mm = pe.matmul
            pe.wait_ge(ld_ctx, 96)
            for g in range(GROUPS):
                for c in range(KC):
                    last = mm(ps_s[0][:, g, 0:B * KEYS], wk_sb[:, c, g * P:(g + 1) * P], ctx_sb[:, c, :],
                              start=c == 0, stop=c == KC - 1)
            last.then_inc(k_psum, 1)
            for b in range(B):
                for c in range(KC):
                    mm(ps_s[1][:, b, 0:D], ctx_sb[:, c, b * KEYS:b * KEYS + P], wv_sb[:, c, :],
                       start=c == 0, stop=c == KC - 1)
                for j in range(4):
                    for c in range(KC):
                        last = mm(ps_s[1][32 * j:32 * j + REM, b, D:2 * D],
                                  ctx_sb[:, c, b * KEYS + P:(b + 1) * KEYS], wv_sb[:, c, :],
                                  start=c == 0, stop=c == KC - 1)
            last.then_inc(v_psum, 1)

            def xn_transposes(t, u):
                pe.wait_ge(xn_made, t + 1)
                if not isinstance(t, int) or t >= 3:
                    pe.wait_ge(OT_made, t - 2)
                for c in range(KC):
                    last = pe.transpose(ps_a[:, c * P:(c + 1) * P], xn[:, u, c * P:(c + 1) * P], id_sb[:, :])
                last.then_inc(xnT_psum, 1)

            def q_product(t, u):
                pe.wait_ge(xnT_made, t + 1)
                for g in range(GROUPS):
                    for c in range(KC):
                        last = mm(ps_a[:, D + g * P:D + (g + 1) * P], wq_sb[:, c, g * P:(g + 1) * P],
                                  xnT[:, u, c, :], start=c == 0, stop=c == KC - 1)
                last.then_inc(q_psum, 1)

            pe.wait_ge(ld_w, 96)
            xn_transposes(0, 0)
            q_product(0, 0)
            pe.wait_ge(kb_made, B * GROUPS * 2)
            pe.wait_ge(v_made, B * 6)

            def scores(t, u, q):
                n = 4 * t + q
                if q == 0:
                    pe.wait_ge(q_split, t + 1)
                if q >= 2 or not isinstance(t, int) or t >= 1:
                    pe.wait_ge(diff_made, n - 1)
                g, j0 = q // 2, 4 * (q % 2)
                for j in range(2):
                    for k, (a, kb) in enumerate(((q_hi, kb_hi), (q_hi, kb_lo), (q_lo, kb_hi))):
                        if isinstance(t, int):
                            rhs = kb[:, t // (TILES // B), g, j0 + 2 * j:j0 + 2 * j + 2, :]
                        else:
                            rhs = kb[:, bass.ds(t // (TILES // B), 1), g, j0 + 2 * j:j0 + 2 * j + 2, :].squeeze(1)
                        last = mm(ps_s[q % 2][:, j, 0:2 * KEYS].rearrange("p (h k) -> p h k", h=2),
                                  a[:, u, g, :], rhs, start=k == 0, stop=k == 2)
                last.then_inc(s_psum, 1)

            def p_transposes(t, k, u):
                if not isinstance(t, int) or 5 * t + k >= 2:
                    pe.wait_ge(t_made, 5 * t + k - 1)
                if k < 4:
                    pe.wait_ge(p_made, 4 * t + k + 1)
                else:
                    pe.wait_ge(pr_made, t + 1)
                for j in range(4):
                    src = pm[u][:, 4 * k + j, :] if k < 4 else \
                        pr[:, u, 4 * j:4 * j + 4, :].rearrange("p h k -> p (h k)")
                    last = pe.transpose(ps_t[(5 * u + k) % 2][:, j * P:(j + 1) * P], src, id_sb[:, :])
                last.then_inc(t_psum, 1)

            def pv(t, u):
                pe.wait_ge(t_made, 5 * t + 5)
                pe.wait_ge(vcur_made, t + 1)
                if not isinstance(t, int) or t < TILES - 2:
                    pe.wait_ge(qf_made, t + 3)
                for g in range(GROUPS):
                    cols = slice(g * P, (g + 1) * P)
                    for a in range(2):
                        qd = 2 * g + a
                        mm(ps_a[64 * a:64 * a + 64, cols], V_cur[:, u, HEADS * 32 + 64 * qd:HEADS * 32 + 64 * qd + 64],
                           PT[:, 4, qd, :], start=True, stop=True, skip_group_check=True)
                    for a in range(2):
                        for r in range(4):
                            h = g * GH + 2 * r + a
                            last = mm(ps_a[32 * r:32 * r + 32, cols], V_cur[:, u, 32 * h:32 * h + 32],
                                      PT[:, h // 4, h % 4, :], start=False, stop=True, skip_group_check=True)
                last.then_inc(pv_psum, 1)
                pe.wait_ge(rden_made, t + 1)
                for g in range(GROUPS):
                    last = pe.transpose(ps_a[:, D + g * P:D + (g + 1) * P],
                                        rden[:, g * GH:(g + 1) * GH, :].rearrange("p h c -> p (h c)"), id_sb[:, :])
                last.then_inc(rT_psum, 1)

            def wo_product(t, u):
                pe.wait_ge(OT_made, t + 1)
                if not isinstance(t, int) or t >= 1:
                    pe.wait_ge(lg_made, t)
                for g in range(GROUPS):
                    last = mm(ps_c[:, 0:D], OT[:, u, g, :], wo_sb[:, g, :], start=g == 0, stop=g == GROUPS - 1)
                last.then_inc(wo_psum, 1)

            def xn2_transposes(t, u):
                pe.wait_ge(xn2_made, t + 1)
                for c in range(KC):
                    last = pe.transpose(ps_c[:, c * P:(c + 1) * P], xn2[:, u, c * P:(c + 1) * P], id_sb[:, :])
                last.then_inc(xn2T_psum, 1)

            def router(t, u):
                pe.wait_ge(xn2T_made, t + 1)
                for c in range(KC):
                    last = mm(ps_c[:, 0:E], xn2T[:, c, :], rw_sb[:, c, :], start=c == 0, stop=c == KC - 1)
                last.then_inc(lg_psum, 1)

            def step(t, u, i, has):
                v = 1 - u
                if has(0):
                    scores(t, u, 0)
                if has(1):
                    xn_transposes(t + 1, v)
                if has(-1):
                    p_transposes(t - 1, 2, v)
                if has(0):
                    scores(t, u, 1)
                if has(1):
                    q_product(t + 1, v)
                if has(-1):
                    p_transposes(t - 1, 3, v)
                    p_transposes(t - 1, 4, v)
                if has(0):
                    scores(t, u, 2)
                if has(-2):
                    xn2_transposes(t - 2, u)
                if has(-1):
                    pv(t - 1, v)
                if has(0):
                    p_transposes(t, 0, u)
                    scores(t, u, 3)
                if has(-2):
                    router(t - 2, u)
                if has(0):
                    p_transposes(t, 1, u)
                if has(-1):
                    wo_product(t - 1, v)
            steps(pe, step)

            pe.wait_ge(pick_made, 1)
            pe.wait_ge(const_made, 3)
            cols = ps_a[:, 0:(TILES + 1) * E].rearrange("p (t e) -> p t e", e=E)
            mm(cols, before_bf[:, :], r_pick[:, :, :], start=True, stop=True)
            for t in range(TILES):
                last = mm(cols[:, t + 1:TILES + 1, :], ones_bf[:, :],
                          r_pick[:, t:t + 1, :].to_broadcast([P, TILES - t, E]),
                          start=False, stop=True, skip_group_check=True)
            last.then_inc(rank_psum, 1)

            def row_transposes(s, u):
                count = s // 4 + 1
                pe.wait_ge(xg_loaded[u], 16 * count)
                if not isinstance(s, int) or s >= 1:
                    pe.wait_ge(xgT_made, s)
                for c in range(KC):
                    last = pe.transpose(ps_c[:, c * P:(c + 1) * P], XG[:, u, c * P:(c + 1) * P], id_sb[:, :])
                last.then_inc(xgT_psum, 1)

            def table(t, s):
                col = t[0:1, s:s + 1] if isinstance(s, int) else t[0:1, bass.ds(s, 1)]
                return col

            big_w1 = big[:, 0:2 * WB].rearrange("p (e w) -> p e w", e=2)[:, :, 0:KC * HID]\
                .rearrange("p e (c h) -> p e c h", c=KC)
            big_w2 = big[:, 0:2 * WB].rearrange("p (e w) -> p e w", e=2)[:, :, KC * HID:WB]\
                .rearrange("p e (j d) -> p e j d", j=HJ)

            def up(s, u, par):
                pe.wait_ge(xgT_made, s + 1)
                if not isinstance(s, int) or s >= 1:
                    pe.wait_ge(hid_made, s)
                for c in range(2):
                    for k in range(KC):
                        last = mm(ps_s[0][:, c, :], xgT[:, u % 2, k, :],
                                  big_w1[:, bass.ds(par, 1), k, 512 * c:512 * (c + 1)].squeeze(1),
                                  start=k == 0, stop=k == KC - 1)
                last.then_inc(up_psum, 1)

            def weights(s):
                e = pe.value_load(table(t_ei, s), min_val=0, max_val=E - 1)
                par = pe.value_load(table(t_par, s), min_val=0, max_val=1)
                pe.wait_ge(w_loaded, 16 * e + 16)
                return par

            def down(s, u, par):
                pe.wait_ge(hidT_made_a, s + 1)
                pe.wait_ge(hidT_made_v, s + 1)
                if not isinstance(s, int) or s >= 2:
                    pe.wait_ge(ys_made, s - 1)
                for j in range(HJ):
                    last = mm(ps_s[1][:, u % 2, 0:D], hidT[:, j, :],
                              big_w2[:, bass.ds(par, 1), j, :].squeeze(1), start=j == 0, stop=j == HJ - 1)
                last.then_inc(down_psum, 1)

            row_transposes(0, 0)
            row_transposes(1, 1)
            pe.wait_ge(tables_made, 1)
            up(0, 0, weights(0))

            def slot(s, u, i, has):
                pe.wait_ge(hid_made, s + 1)
                for j in range(HJ):
                    last = pe.transpose(ps_t[j // 4][:, (j % 4) * P:(j % 4 + 1) * P], hid[:, j * P:(j + 1) * P],
                                        id_sb[:, :])
                last.then_inc(hidT_psum, 1)
                par = pe.value_load(table(t_par, s), min_val=0, max_val=1)
                if has(2):
                    row_transposes(s + 2, (u + 2) % 4)
                if has(1):
                    up(s + 1, (u + 1) % 4, weights(s + 1))
                down(s, u, par)
            ff_slots(pe, slot)


def kernel(x, ctx_1024, L0_xattn_Wq, L0_xattn_bq, L0_xattn_Wk, L0_xattn_bk, L0_xattn_Wv, L0_xattn_bv,
           L0_xattn_Wo, L0_xattn_bo, L0_ffn_router_w, L0_ffn_w1, L0_ffn_w2):
    import concourse.bacc as _bacc
    from concourse.bass_utils import run_bass_kernel_spmd as _run

    def laid(a, *order):
        return np.ascontiguousarray(np.asarray(a).transpose(*order)) if order else np.asarray(a)

    w1 = laid(L0_ffn_w1, 0, 2, 1).reshape(E, KC, P, HID).transpose(0, 2, 1, 3).reshape(E, P, KC * HID)
    w2 = laid(L0_ffn_w2, 0, 2, 1).reshape(E, HJ, P, D).transpose(0, 2, 1, 3).reshape(E, P, HJ * D)
    lanes = np.arange(P)
    data = {
        "x": laid(x).reshape(TOK, D),
        "ctxT": laid(ctx_1024, 2, 0, 1).reshape(D, B * KEYS),
        "wq": laid(L0_xattn_Wq, 1, 0, 2).reshape(D, D),
        "bq": laid(L0_xattn_bq).reshape(D),
        "wk": laid(L0_xattn_Wk, 1, 0, 2).reshape(D, D),
        "bk": laid(L0_xattn_bk).reshape(D),
        "wv": laid(L0_xattn_Wv, 1, 0, 2).reshape(D, D),
        "bv": laid(L0_xattn_bv).reshape(D),
        "wo": laid(L0_xattn_Wo),
        "bo": laid(L0_xattn_bo),
        "rwT": laid(L0_ffn_router_w, 1, 0),
        "wexp": np.concatenate([w1, w2], axis=2),
        "ident": np.eye(P, dtype=np.float32),
        "headmask": (lanes[:, None] // DK == np.arange(GH)[None]).astype(np.float32),
        "before": (lanes[:, None] < lanes[None]).astype(np.float32),
        "em8": np.broadcast_to(np.arange(E) - float(E), (P, E)).astype(np.float32),
        "tokid": (np.arange(TILES + 1)[None] * P + lanes[:, None]).astype(np.int32),
        "slots": np.concatenate([np.arange(SLOTS)[None] * P + lanes[:, None],
                                 np.arange(SLOTS)[None]]).astype(np.float32),
    }
    nc = _bacc.Bacc("TRN2", target_bir_lowering=False, num_devices=1)
    arrays, args = {}, []
    for name, a in data.items():
        arrays[f"in_{name}"] = np.ascontiguousarray(a)
        args.append(nc.dram_tensor(f"in_{name}", a.shape, mybir.dt.from_np(a.dtype), kind="ExternalInput").ap())
    args.append(nc.dram_tensor("result", [TOK + P, D], mybir.dt.float32, kind="ExternalOutput").ap())
    xattn_moe_kernel(nc, *args)
    r = _run(nc, [arrays], core_ids=[0])
    return r.results[0]["result"][0:TOK].reshape(B, S, D)
```

```python
import numpy as np
import concourse.bass as bass
from concourse import mybir
from contextlib import ExitStack

B, S, D = 2, 1024, 256
KEYS = 154
HEADS, DK = 16, 16
E, HID = 8, 1024
TOK = B * S
P = 128
TILES = TOK // P
KC = D // P
REM = KEYS - P
GH = P // DK
GROUPS = HEADS // GH
QUADS = HEADS // 4
SLOTS = (2 * TOK + E * (P - 1)) // P
ROW = D + 4
HJ = HID // P
WB = KC * HID + HJ * D
VW = HEADS * 32 + QUADS * 64
EPS = 1e-5


def xattn_moe_kernel(nc, x, ctxT, wq, bq, wk, bk, wv, bv, wo, bo, rwT, wexp,
                     ident, headmask, before, em8, tokid, slots, out):
    fp32, f32r = mybir.dt.float32, mybir.dt.float32r
    bf16, i32 = mybir.dt.bfloat16, mybir.dt.int32
    ALU, ACT, AX = mybir.AluOpType, mybir.ActivationFunctionType, mybir.AxisListType

    routed = nc.dram_tensor("routed", [SLOTS * P, ROW], fp32).ap()

    with ExitStack() as ctx:
        def sb(name, shape, dt=fp32):
            return ctx.enter_context(nc.sbuf_tensor(name, shape, dt))

        def sem(name):
            return ctx.enter_context(nc.semaphore(name))

        id_sb = sb("id_sb", [P, P])
        mask_sb = sb("mask_sb", [P, GH])
        before_sb = sb("before_sb", [P, P])
        before_bf = sb("before_bf", [P, P], bf16)
        ones_bf = sb("ones_bf", [P, P], bf16)
        em8_sb = sb("em8_sb", [P, E])
        tokid_sb = sb("tokid_sb", [P, TILES + 1], i32)
        slots_sb = sb("slots_sb", [P, SLOTS])
        slotno_sb = sb("slotno_sb", [1, SLOTS])
        wq_sb = sb("wq_sb", [P, KC, D])
        wo_sb = sb("wo_sb", [P, KC, D])
        rw_sb = sb("rw_sb", [P, KC, E])
        bq_sb = sb("bq_sb", [P, GROUPS])
        bq4_sb = sb("bq4_sb", [P, GROUPS])
        bk_sb = sb("bk_sb", [P, GROUPS])
        bv_sb = sb("bv_sb", [P, D])
        bo_sb = sb("bo_sb", [P, D])
        half_sb = sb("half_sb", [P, 1])
        xs = sb("xs", [P, TILES, D])
        XR = sb("XR", [P, TILES, ROW])
        LG = sb("LG", [P, TILES, E])
        KBN = B * GROUPS * GH * KEYS
        KB = sb("KB", [P, 2 * 2 * WB], f32r)
        WS = KB[:, :].rearrange("p (e s w) -> p e s w", e=2, s=2)
        kb_hi = KB[:, 0:KBN].rearrange("p (b g j k) -> p b g j k", b=B, g=GROUPS, j=GH)
        kb_lo = KB[:, KBN:2 * KBN].rearrange("p (b g j k) -> p b g j k", b=B, g=GROUPS, j=GH)
        V_all = sb("V_all", [P, B, VW])
        V_cur = sb("V_cur", [P, 2, VW])
        big = sb("big", [P, 2 * (HEADS * KEYS + HEADS * P)])
        DSZ = HEADS * KEYS
        diff = [big[:, u * DSZ:(u + 1) * DSZ].rearrange("p (h k) -> p h k", h=HEADS) for u in range(2)]
        o1 = 2 * DSZ
        pm = [big[:, o1 + u * HEADS * P:o1 + (u + 1) * HEADS * P].rearrange("p (h k) -> p h k", h=HEADS)
              for u in range(2)]
        o2 = o1 + 2 * HEADS * P
        ctx_sb = big[:, 0:KC * B * KEYS].rearrange("p (c n) -> p c n", c=KC)
        wk_sb = big[:, 1024:1024 + KC * D].rearrange("p (c n) -> p c n", c=KC)
        wv_sb = big[:, 2048:2048 + KC * D].rearrange("p (c n) -> p c n", c=KC)
        KT = big[:, 3072:3072 + GROUPS * B * KEYS].rearrange("p (g n) -> p g n", g=GROUPS)
        o3 = 2 * KBN
        KTr = KB[:, o3:o3 + 2 * GROUPS * B * KEYS].rearrange("p (s g n) -> p s g n", s=2, g=GROUPS)
        wraw = big[:, 0:WB]
        pr = sb("pr", [P, 2, HEADS, 32])
        PT = sb("PT", [P, 5, 4, P])
        half = sb("half", [P, 4, 64])
        fold = sb("fold", [P, 2, HEADS, 32])
        st1 = sb("st1", [P, 2, 6])
        mv1 = sb("mv1", [P, 2, 4])
        xn = sb("xn", [P, 2, D])
        xnT = sb("xnT", [P, 2, KC, P])
        qf = sb("qf", [P, 2, GROUPS, P])
        o4 = o3 + 2 * GROUPS * B * KEYS
        q_hi = KB[:, o4:o4 + 2 * D].rearrange("p (u g n) -> p u g n", u=2, g=GROUPS)
        q_lo = KB[:, o4 + 2 * D:o4 + 4 * D].rearrange("p (u g n) -> p u g n", u=2, g=GROUPS)
        mx = sb("mx", [P, 2, 4])
        den = sb("den", [P, HEADS])
        rec = sb("rec", [P, HEADS])
        rden = sb("rden", [P, HEADS, DK])
        rT = sb("rT", [P, GROUPS, P])
        OT = sb("OT", [P, 2, GROUPS, P])
        xb = sb("xb", [P, 2, D])
        x1 = sb("x1", [P, 2, D])
        st2 = sb("st2", [P, 2, 6])
        mv2 = sb("mv2", [P, 2, 4])
        xn2 = sb("xn2", [P, 2, D])
        xn2T = sb("xn2T", [P, KC, P])
        fill = sb("fill", [P, ROW])
        zero = sb("zero", [P, D])
        r_a, r_b = (half[:, 2 * u:2 * u + 2, :].rearrange("p a (t e) -> p (a t) e", e=E) for u in range(2))
        r_o1, r_o2, r_ex = (fold[:, 0, 4 * n:4 * n + 4, :].rearrange("p a (t e) -> p (a t) e", e=E)
                            for n in range(3))
        r_m1 = sb("r_m1", [P, TILES])
        r_m2 = sb("r_m2", [P, TILES])
        r_c = sb("r_c", [P, TILES])
        r_e2 = sb("r_e2", [P, TILES])
        r_s = sb("r_s", [P, TILES])
        r_pick = sb("r_pick", [P, TILES + 1, E], bf16)
        r_rank = sb("r_rank", [P, TILES + 1, E])
        r_i = sb("r_i", [P, E], i32)
        r_i2 = sb("r_i2", [P, E], i32)
        r_n = sb("r_n", [P, E])
        r_p = sb("r_p", [P, 2, 4 + E])
        r_st = sb("r_st", [P, E])
        r_base = sb("r_base", [P, E])
        r_pos = sb("r_pos", [P, 2, TILES])
        pos_i = sb("pos_i", [P, 2, TILES], i32)
        t_cmp = sb("t_cmp", [1, SLOTS, E])
        t_e = sb("t_e", [1, SLOTS])
        t_ei = sb("t_ei", [1, SLOTS], i32)
        t_first = sb("t_first", [1, SLOTS])
        t_next = sb("t_next", [1, SLOTS], i32)
        XG = big[:, WB:WB + 4 * ROW].rearrange("p (u c) -> p u c", u=4)
        xgT = sb("xgT", [P, 2, 2, KC, P], f32r)
        wrow = sb("wrow", [P, 4, 4])
        rowtok = sb("rowtok", [P, 4], i32)
        hid = big[:, WB + 4 * ROW:WB + 4 * ROW + HID]
        hidT = sb("hidT", [P, 2, HJ, P], f32r)
        o5 = WB + 4 * ROW + HID
        ys = big[:, o5:o5 + 2 * D].rearrange("p (u d) -> p u d", u=2)

        ps_s = [ctx.enter_context(nc.psum_tensor(f"ps_s{u}", [P, 2, 512], fp32)) for u in range(2)]
        ps_t = [ctx.enter_context(nc.psum_tensor(f"ps_t{u}", [P, 512], fp32)) for u in range(2)]
        ps_a = ctx.enter_context(nc.psum_tensor("ps_a", [P, 512], fp32))
        ps_c = ctx.enter_context(nc.psum_tensor("ps_c", [P, 512], fp32))

        ld_ctx, ld_w, ld_c, ld_x0, ld_x1 = (sem(n) for n in ("ld_ctx", "ld_w", "ld_c", "ld_x0", "ld_x1"))
        fill_made, fill_stored = sem("fill_made"), sem("fill_stored")
        const_made, v_zeroed, p_zeroed = sem("const_made"), sem("v_zeroed"), sem("p_zeroed")
        bq_made = sem("bq_made")
        k_psum, k_made, kt_hi, kt_lo, kb_made = (sem(n) for n in ("k_psum", "k_made", "kt_hi", "kt_lo", "kb_made"))
        v_psum, v_made = sem("v_psum"), sem("v_made")
        st1_made, mv1_made, var1_made, rstd1_made = (sem(n) for n in ("st1_made", "mv1_made", "var1_made", "rstd1_made"))
        xn_made, xnT_psum, xnT_made = sem("xn_made"), sem("xnT_psum"), sem("xnT_made")
        q_psum, qf_made, q_hi_made, q_split = sem("q_psum"), sem("qf_made"), sem("q_hi_made"), sem("q_split")
        s_psum, mx_made, diff_made, p_made, pr_made = (sem(n) for n in ("s_psum", "mx_made", "diff_made", "p_made", "pr_made"))
        t_psum, t_made = sem("t_psum"), sem("t_made")
        half_made, fold_made, den_made, rec_made, rden_made = (sem(n) for n in
            ("half_made", "fold_made", "den_made", "rec_made", "rden_made"))
        pv_psum, rT_psum, rT_made, OT_made = (sem(n) for n in ("pv_psum", "rT_psum", "rT_made", "OT_made"))
        xb_made, wo_psum, x1_made = sem("xb_made"), sem("wo_psum"), sem("x1_made")
        vcur_made = [sem(f"vcur_made{u}") for u in range(2)]
        x1_stored = [sem(f"x1_stored{u}") for u in range(2)]
        xr_stored = [sem(f"xr_stored{u}") for u in range(2)]
        st2_made, mv2_made, var2_made, rstd2_made, xn2_made = (sem(n) for n in ("st2_made", "mv2_made", "var2_made", "rstd2_made", "xn2_made"))
        xn2T_psum, xn2T_made, lg_psum, lg_made = (sem(n) for n in ("xn2T_psum", "xn2T_made", "lg_psum", "lg_made"))
        r_step, r_shift, r_exp, pick_made, rank_psum = (sem(n) for n in ("r_step", "r_shift", "r_exp", "pick_made", "rank_psum"))
        rows_made, tables_made, scattered = sem("rows_made"), sem("tables_made"), sem("scattered")
        w_loaded, w_hi, w_lo = sem("w_loaded"), sem("w_hi"), sem("w_lo")
        xg_loaded = [sem(f"xg_loaded{u}") for u in range(4)]
        xgT_psum, xgT_made, wr1, wr2, wr3, wrow_made = (sem(n) for n in ("xgT_psum", "xgT_made", "wr1", "wr2", "wr3", "wrow_made"))
        up_psum, hid_made, hidT_psum, hidT_hi, hidT_lo, xgT_hi = (sem(n) for n in
            ("up_psum", "hid_made", "hidT_psum", "hidT_hi", "hidT_lo", "xgT_hi"))
        down_psum, ys_made, added = sem("down_psum"), sem("ys_made"), sem("added")

        dve_passed, pool_passed = sem("dve_passed"), sem("pool_passed")

        block = ctx.enter_context(nc.Block())

        LOOP0, LOOP1 = 4, TILES - 2

        def steps(eng, step):
            for t in range(LOOP0):
                step(t, t % 2, t // 2, lambda d, t=t: 0 <= t + d < TILES)
            with eng.Fori(LOOP0 // 2, LOOP1 // 2) as i:
                for u in range(2):
                    step(2 * i + u, u, i, lambda d: True)
            for t in range(LOOP1, TILES + 2):
                step(t, t % 2, t // 2, lambda d, t=t: 0 <= t + d < TILES)

        HALVES = 2
        WH = WB // HALVES
        FF_LOOP = (SLOTS - 4) // 4 * 4

        def ff_slots(eng, slot):
            for s in range(4):
                slot(s, s, 0, lambda d: True)
            with eng.Fori(1, FF_LOOP // 4) as i:
                for u in range(4):
                    slot(4 * i + u, u, i, lambda d: True)
            for s in range(FF_LOOP, SLOTS):
                slot(s, s % 4, s // 4, lambda d, s=s: s + d < SLOTS)

        def table(t, s):
            return t[0:1, s:s + 1] if isinstance(s, int) else t[0:1, bass.ds(s, 1)]

        def s_after_first(s):
            return not isinstance(s, int) or s >= 1

        @block.sync
        def _(sp):
            sp.dma_start(ctx_sb, ctxT.rearrange("(c p) n -> p c n", p=P)).then_inc(ld_ctx, 16)
            sp.dma_start(wk_sb, wk.rearrange("(c p) n -> p c n", p=P)).then_inc(ld_ctx, 16)
            sp.dma_start(wv_sb, wv.rearrange("(c p) n -> p c n", p=P)).then_inc(ld_ctx, 16)
            sp.dma_start(bk_sb[:, :], bk.rearrange("(g p) -> p g", p=P),
                         allow_slow_non_contiguous=True).then_inc(ld_ctx, 16)
            sp.dma_start(bv_sb[:, :], bv.unsqueeze(0).to_broadcast([P, D])).then_inc(ld_ctx, 16)
            sp.dma_start(mask_sb[:, :], headmask).then_inc(ld_ctx, 16)
            sp.dma_start(before_sb[:, :], before).then_inc(ld_c, 16)
            sp.dma_start(em8_sb[:, :], em8).then_inc(ld_c, 16)
            sp.dma_start(tokid_sb[:, :], tokid).then_inc(ld_c, 16)
            sp.dma_start(slots_sb[:, :], slots[0:P, :]).then_inc(ld_c, 16)
            sp.dma_start(slotno_sb[:, :], slots[P:P + 1, :]).then_inc(ld_c, 16)
            sp.wait_ge(fill_made, 3)
            sp.dma_start(routed.rearrange("(s p) c -> p s c", p=P),
                         fill[:, :].unsqueeze(1).to_broadcast([P, SLOTS, ROW])).then_inc(fill_stored, 16)
            sp.dma_start(out[TOK:TOK + P, :], zero[:, :]).then_inc(fill_stored, 16)

            sp.wait_ge(v_made, B * 6)

            def step(t, u, i, has):
                if has(0):
                    if not isinstance(t, int) or t >= 2:
                        sp.wait_ge(pv_psum, t - 1)
                    src = V_all[:, t // (TILES // B), :] if isinstance(t, int) else \
                        V_all[:, bass.ds(t // (TILES // B), 1), :].squeeze(1)
                    sp.dma_start(V_cur[:, u, :], src).then_inc(vcur_made[u], 16)
                if has(-2):
                    sp.wait_ge(x1_made, t - 1)
                    sp.dma_start(out[bass.ds((t - 2) * P, P), :], x1[:, u, :]).then_inc(x1_stored[u], 16)
                    sp.wait_ge(xn2_made, t - 1)
                    sp.dma_start(XR[:, bass.ds(t - 2, 1), 0:D], xn2[:, u:u + 1, :]).then_inc(xr_stored[u], 16)
            steps(sp, step)

            sp.wait_ge(t_psum, 5 * TILES)
            sp.wait_ge(fold_made, 5 * TILES)
            for e in range(E):
                if e:
                    sp.wait_ge(w_lo, HALVES * e)
                sp.dma_start(wraw, wexp[e]).then_inc(w_loaded, 16)
            sp.wait_ge(added, 16 * SLOTS)

        @block.gpsimd
        def _(pool):
            pool.memset(half_sb[:, :], -0.5).then_inc(const_made, 1)
            pool.memset(fill[:, :], 0.0).then_inc(fill_made, 1)
            pool.memset(zero[:, :], 0.0)
            pool.memset(V_all[:, :, :], 0.0).then_inc(v_zeroed, 1)
            pool.memset(pr[:, :, :, :], 0.0).then_inc(p_zeroed, 1)
            pool.memset(ones_bf[:, :], 1.0).then_inc(const_made, 1)
            pool.wait_ge(ld_c, 80)
            pool.wait_ge(fill_made, 1)
            pool.tensor_copy(fill[:, D:D + 1].bitcast(i32), tokid_sb[:, TILES:TILES + 1]).then_inc(fill_made, 1)
            pool.memset(fill[:, ROW - 1:ROW], -1.0).then_inc(fill_made, 1)
            pool.tensor_copy(XR[:, :, D].bitcast(i32), tokid_sb[:, 0:TILES]).then_inc(const_made, 1)
            pool.wait_ge(const_made, 3)

            def wait_alone(s, n):
                pool.wait_ge(s, n)
                if not isinstance(n, int):
                    pool.sem_inc(pool_passed, 1)

            def rstd(t, u, stats, made, rstd_made):
                pool.wait_ge(made, t + 1)
                pool.tensor_tensor(stats[:, u, 3:4], stats[:, u, 2:3], half_sb[:, :], ALU.pow).then_inc(rstd_made, 1)

            def xs_tile(t):
                return xs[:, bass.ds(t, 1), :].squeeze(1) if not isinstance(t, int) else xs[:, t, :]

            def split_q(t, u):
                pool.wait_ge(q_hi_made, t + 1)
                if not isinstance(t, int) or t >= 2:
                    wait_alone(s_psum, 4 * (t - 1))
                pool.tensor_tensor(q_lo[:, u, :, :], qf[:, u, :, :], q_hi[:, u, :, :].bitcast(fp32),
                                   ALU.subtract).then_inc(q_split, 1)

            def fold_quad(t, u, q):
                pool.wait_ge(p_made, 4 * t + q + 1)
                if q == 0 and (not isinstance(t, int) or t >= 2):
                    pool.wait_ge(den_made, t - 1)
                heads = slice(4 * q, 4 * q + 4)
                if q or not isinstance(t, int) or t >= 1:
                    pool.wait_ge(fold_made, 5 * t + q)
                pool.tensor_tensor(half[:, :, :], pm[u][:, heads, 0:64], pm[u][:, heads, 64:128],
                                   ALU.add).then_inc(half_made, 1)
                pool.wait_ge(half_made, 4 * t + q + 1)
                pool.tensor_tensor(fold[:, u, heads, :], half[:, :, 0:32], half[:, :, 32:64],
                                   ALU.add).then_inc(fold_made, 1)

            def fold_rest(t, u):
                pool.wait_ge(pr_made, t + 1)
                pool.wait_ge(fold_made, 5 * t + 4)
                pool.tensor_tensor(fold[:, u, :, :], fold[:, u, :, :], pr[:, u, :, :], ALU.add).then_inc(fold_made, 1)

            rstd(0, 0, mv1, var1_made, rstd1_made)
            rstd(1, 1, mv1, var1_made, rstd1_made)
            split_q(0, 0)
            pool.wait_ge(v_made, B * 6)

            def step(t, u, i, has):
                v = 1 - u
                if has(-1):
                    fold_quad(t - 1, v, 3)
                    fold_rest(t - 1, v)
                if has(-2):
                    rstd(t - 2, u, mv2, var2_made, rstd2_made)
                if has(0):
                    fold_quad(t, u, 0)
                if has(1):
                    split_q(t + 1, v)
                if has(0):
                    fold_quad(t, u, 1)
                if has(2):
                    rstd(t + 2, u, mv1, var1_made, rstd1_made)
                if has(-1):
                    if not isinstance(t, int) or t >= 3:
                        pool.wait_ge(x1_made, t - 2)
                    pool.tensor_tensor(xb[:, v, :], xs_tile(t - 1), bo_sb[:, :], ALU.add).then_inc(xb_made, 1)
                if has(0):
                    fold_quad(t, u, 2)

            pool.wait_ge(ld_w, 16 * 6)
            steps(pool, step)

            pool.wait_ge(rows_made, 1)
            pool.wait_ge(fill_stored, 32)
            for u in range(2):
                pool.wait_ge(xr_stored[u], 16 * TILES // 2)
            for t in range(TILES):
                for k in range(2):
                    pool.indirect_dma_start(routed, bass.IndirectOffsetOnAxis(pos_i[:, k, t:t + 1], 0),
                                            XR[:, t, :], None).then_inc(scattered, 16)
            pool.wait_ge(scattered, 16 * 2 * TILES)
            for u in range(2):
                pool.wait_ge(x1_stored[u], 16 * TILES // 2)


            def slot(s, u, i, has):
                wait_alone(ys_made, s + 1)
                if not isinstance(s, int) or s >= 1:
                    wait_alone(added, 16 * s)
                pool.indirect_dma_start(out, bass.IndirectOffsetOnAxis(rowtok[:, u:u + 1], 0),
                                        ys[:, u % 2, :], None, compute_op=ALU.add).then_inc(added, 16)
            ff_slots(pool, slot)

        @block.scalar
        def _(act):
            def to_cols(v, ap):
                return act.dma_start(ap, v.rearrange("(g p) -> p g", p=P), allow_slow_non_contiguous=True)
            xv = x.rearrange("(t p) d -> p t d", p=P)
            act.dma_start(xs[:, 0:4, :], xv[:, 0:4, :]).then_inc(ld_x0, 16)
            act.dma_start(id_sb[:, :], ident).then_inc(ld_w, 16)
            act.dma_start(wq_sb[:, :, :], wq.rearrange("(c p) n -> p c n", p=P)).then_inc(ld_w, 16)
            to_cols(bq, bq_sb[:, :]).then_inc(ld_w, 16)
            act.dma_start(xs[:, 4:TILES, :], xv[:, 4:TILES, :]).then_inc(ld_x1, 16)
            act.dma_start(wo_sb[:, :, :], wo.rearrange("(c p) n -> p c n", p=P)).then_inc(ld_w, 16)
            act.dma_start(rw_sb[:, :, :], rwT.rearrange("(c p) n -> p c n", p=P)).then_inc(ld_w, 16)
            act.dma_start(bo_sb[:, :], bo.unsqueeze(0).to_broadcast([P, D])).then_inc(ld_w, 16)
            act.wait_ge(ld_w, 96)
            act.mul(bq4_sb[:, :], bq_sb[:, :], DK ** -0.5).then_inc(bq_made, 1)
            act.wait_ge(bq_made, 1)

            def evac_xnT(t, u):
                act.wait_ge(xnT_psum, t + 1)
                if not isinstance(t, int) or t >= 2:
                    act.wait_ge(q_psum, t - 1)
                act.activation(xnT[:, u, :, :], ps_a[:, 0:KC * P].rearrange("p (c n) -> p c n", c=KC),
                               ACT.Copy).then_inc(xnT_made, 1)

            def evac_q(t, u):
                act.wait_ge(q_psum, t + 1)
                if not isinstance(t, int) or t >= 2:
                    act.wait_ge(q_split, t - 1)
                for g in range(GROUPS):
                    last = act.activation(qf[:, u, g, :], ps_a[:, D + g * P:D + (g + 1) * P], ACT.Identity,
                                          bias=bq4_sb[:, g:g + 1], scale=DK ** -0.5)
                last.then_inc(qf_made, 1)
                if not isinstance(t, int) or t >= 2:
                    act.wait_ge(s_psum, 4 * (t - 1))
                act.wait_ge(qf_made, t + 1)
                act.activation(q_hi[:, u, :, :], qf[:, u, :, :], ACT.Copy).then_inc(q_hi_made, 1)

            evac_xnT(0, 0)
            evac_q(0, 0)
            act.wait_ge(p_zeroed, 1)
            act.wait_ge(kb_made, B * GROUPS * 2)

            def exp(t, u, q):
                act.wait_ge(diff_made, 4 * t + q + 1)
                if q == 0 and (not isinstance(t, int) or t >= 2):
                    act.wait_ge(fold_made, 5 * (t - 1))
                    act.wait_ge(t_psum, 5 * (t - 1))
                act.activation(pm[u][:, 4 * q:4 * q + 4, :], diff[u][:, 4 * q:4 * q + 4, 0:P],
                               ACT.Exp).then_inc(p_made, 1)

            def evac_t(t, k, u):
                act.wait_ge(t_psum, 5 * t + k + 1)
                if not isinstance(t, int) or t >= 1:
                    act.wait_ge(pv_psum, t)
                act.activation(PT[:, k, :, :], ps_t[(5 * u + k) % 2][:, :].rearrange("p (a n) -> p a n", a=4),
                               ACT.Copy).then_inc(t_made, 1)

            def step(t, u, i, has):
                v = 1 - u
                if has(-1):
                    evac_t(t - 1, 2, v)
                if has(1):
                    evac_xnT(t + 1, v)
                if has(-1):
                    evac_t(t - 1, 3, v)
                if has(0):
                    exp(t, u, 0)
                if has(-1):
                    evac_t(t - 1, 4, v)
                if has(1):
                    evac_q(t + 1, v)
                if has(0):
                    exp(t, u, 1)
                if has(-2):
                    act.wait_ge(xn2T_psum, t - 1)
                    if not isinstance(t, int) or t >= 3:
                        act.wait_ge(lg_psum, t - 2)
                    act.activation(xn2T[:, :, :], ps_c[:, 0:KC * P].rearrange("p (c n) -> p c n", c=KC),
                                   ACT.Copy).then_inc(xn2T_made, 1)
                if has(0):
                    exp(t, u, 2)
                if has(-1):
                    act.wait_ge(rT_psum, t)
                    if not isinstance(t, int) or t >= 2:
                        act.wait_ge(OT_made, t - 1)
                    act.activation(rT[:, :, :], ps_a[:, D:2 * D].rearrange("p (g n) -> p g n", g=GROUPS),
                                   ACT.Copy).then_inc(rT_made, 1)
                if has(0):
                    evac_t(t, 0, u)
                    evac_t(t, 1, u)
                    exp(t, u, 3)
                    act.activation(pr[:, u, :, 0:REM], diff[u][:, :, P:KEYS], ACT.Exp).then_inc(pr_made, 1)
            steps(act, step)

            act.wait_ge(r_shift, 1)
            act.activation(r_ex[:, :, :], r_a[:, :, :], ACT.Exp).then_inc(r_exp, 1)
            act.wait_ge(r_shift, 2)
            act.activation(r_e2[:, :], r_s[:, :], ACT.Exp).then_inc(r_exp, 1)

            def split_weights(e, par, n):
                act.wait_ge(w_loaded, 16 * e + 16)
                dst = WS[:, par, 0, n * WH:(n + 1) * WH] if isinstance(par, int) else \
                    WS[:, bass.ds(par, 1), 0, n * WH:(n + 1) * WH].squeeze(1)
                act.activation(dst, wraw[:, n * WH:(n + 1) * WH], ACT.Copy).then_inc(w_hi, 1)
            for e in range(2):
                for n in range(HALVES):
                    split_weights(e, e, n)

            def gelu(s):
                act.wait_ge(up_psum, s + 1)
                if not isinstance(s, int) or s >= 1:
                    act.wait_ge(hidT_psum, s)
                act.activation(hid.rearrange("p (c n) -> p c n", c=2), ps_s[0][:, :, :],
                               ACT.Gelu).then_inc(hid_made, 1)

            def load_rows(s, u):
                act.dma_start(XG[:, u, :], routed[bass.ds(s * P, P), :]).then_inc(xg_loaded[u], 16)
            act.wait_ge(scattered, 16 * 2 * TILES)
            for s in range(4):
                load_rows(s, s)
            act.wait_ge(tables_made, 1)
            gelu(0)

            def slot(s, u, i, has):
                if has(4):
                    act.wait_ge(xgT_made, s + 1)
                    act.wait_ge(wrow_made, s + 1)
                    load_rows(s + 4, u)
                if has(1) and s_after_first(s):
                    to_split = act.value_load(table(t_next, s), min_val=0, max_val=E - 1)
                act.wait_ge(hidT_psum, s + 1)
                if not isinstance(s, int) or s >= 1:
                    act.wait_ge(down_psum, s)
                for a in range(2):
                    act.activation(hidT[:, 0, 4 * a:4 * a + 4, :], ps_t[a][:, :].rearrange("p (a n) -> p a n", a=4),
                                   ACT.Copy).then_inc(hidT_hi, 1)
                if has(1) and s_after_first(s):
                    with act.If(to_split > 0):
                        split_weights(to_split, to_split % 2, 0)
                if has(1):
                    gelu(s + 1)
                if has(1) and s_after_first(s):
                    with act.If(to_split > 0):
                        split_weights(to_split, to_split % 2, 1)
            ff_slots(act, slot)

        @block.vector
        def _(dve):
            dve.wait_ge(ld_x0, 16)

            def wait_alone(s, n):
                dve.wait_ge(s, n)
                if not isinstance(n, int):
                    dve.sem_inc(dve_passed, 1)

            def x_tile(t):
                return xs[:, t, :] if isinstance(t, int) else xs[:, bass.ds(t, 1), :].squeeze(1)

            def sums1(t, u):
                if not isinstance(t, int) or t >= 2:
                    dve.wait_ge(xn_made, t - 1)
                dve.bn_stats(st1[:, u, :], x_tile(t)).then_inc(st1_made, 1)

            def aggregate(t, u, st, st_made, mv, mv_made):
                wait_alone(st_made, t + 1)
                dve.bn_aggr(mv[:, u, 0:2], st[:, u, :]).then_inc(mv_made, 1)

            def add_eps(t, u, mv, mv_made, var_made):
                dve.wait_ge(mv_made, t + 1)
                dve.tensor_scalar(mv[:, u, 2:3], mv[:, u, 1:2], EPS, None, ALU.add).then_inc(var_made, 1)

            def norm1(t, u):
                dve.wait_ge(rstd1_made, t + 1)
                if not isinstance(t, int) or t >= 2:
                    dve.wait_ge(xnT_psum, t - 1)
                dve.tensor_scalar(xn[:, u, :], x_tile(t), mv1[:, u, 0:1], mv1[:, u, 3:4],
                                  ALU.subtract, ALU.mult).then_inc(xn_made, 1)

            def norm2(t, u, i):
                dve.wait_ge(rstd2_made, t + 1)
                if not isinstance(t, int) or t >= 2:
                    dve.wait_ge(xr_stored[u], 16 * i)
                    dve.wait_ge(xn2T_psum, t - 1)
                dve.tensor_scalar(xn2[:, u, :], x1[:, u, :], mv2[:, u, 0:1], mv2[:, u, 3:4],
                                  ALU.subtract, ALU.mult).then_inc(xn2_made, 1)
            for t in range(2):
                sums1(t, t)
                aggregate(t, t, st1, st1_made, mv1, mv1_made)
                add_eps(t, t, mv1, mv1_made, var1_made)
            norm1(0, 0)
            norm1(1, 1)

            dve.wait_ge(ld_ctx, 96)
            dve.wait_ge(k_psum, 1)
            for g in range(GROUPS):
                dve.tensor_scalar(KT[:, g, :], ps_s[0][:, g, 0:B * KEYS], bk_sb[:, g:g + 1], None,
                                  ALU.add).then_inc(k_made, 1)
            dve.wait_ge(k_made, 2)
            dve.tensor_copy(KTr[:, 0, :, :], KT).then_inc(kt_hi, 1)
            dve.wait_ge(kt_hi, 1)
            dve.tensor_tensor(KTr[:, 1, :, :], KT, KTr[:, 0, :, :].bitcast(fp32), ALU.subtract).then_inc(kt_lo, 1)
            dve.wait_ge(kt_lo, 1)
            for b in range(B):
                for g in range(GROUPS):
                    for part, kb in ((0, kb_hi), (1, kb_lo)):
                        src = KTr[:, part, g, b * KEYS:(b + 1) * KEYS].bitcast(fp32)
                        dve.tensor_tensor(kb[:, b, g, :, :], src.unsqueeze(1).to_broadcast([P, GH, KEYS]),
                                          mask_sb[:, :].unsqueeze(2).to_broadcast([P, GH, KEYS]),
                                          ALU.mult).then_inc(kb_made, 1)
            dve.wait_ge(v_psum, 1)
            dve.wait_ge(v_zeroed, 1)
            for b in range(B):
                vm = V_all[:, b, 0:HEADS * 32].rearrange("p (r a c) -> p r a c", a=2, c=32)
                vr = V_all[:, b, HEADS * 32:VW].rearrange("p (q c) -> p q c", c=64)
                main = ps_s[1][:, b, 0:D].rearrange("p (r a c) -> p r a c", a=2, c=DK)
                bvm = bv_sb[:, :].rearrange("p (r a c) -> p r a c", a=2, c=DK)
                for a in range(2):
                    dve.tensor_tensor(vm[:, :, a, DK * a:DK * a + DK], main[:, :, a, :], bvm[:, :, a, :],
                                      ALU.add).then_inc(v_made, 1)
                for j in range(4):
                    lanes = slice(32 * j, 32 * j + REM)
                    rest = ps_s[1][lanes, b, D:2 * D].rearrange("p (q j c) -> p q j c", j=4, c=DK)
                    bvr = bv_sb[lanes, :].rearrange("p (q j c) -> p q j c", j=4, c=DK)
                    dve.tensor_tensor(vr[lanes, :, DK * j:DK * j + DK], rest[:, :, j, :], bvr[:, :, j, :],
                                      ALU.add).then_inc(v_made, 1)

            dve.wait_ge(ld_x1, 16)
            dve.wait_ge(kb_made, B * GROUPS * 2)

            def split_heads(q):
                return ps_s[q % 2][:, :, 0:2 * KEYS].rearrange("p b (h k) -> p b h k", h=2), \
                    mx[:, q % 2, :].rearrange("p (b h) -> p b h", b=2)

            def maxima(t, q):
                dve.wait_ge(s_psum, 4 * t + q + 1)
                src, m = split_heads(q)
                dve.tensor_reduce(m, src, AX.X, ALU.max).then_inc(mx_made, 1)

            def shift(t, u, q):
                dve.wait_ge(mx_made, 4 * t + q + 1)
                if q == 0 and (not isinstance(t, int) or t >= 2):
                    dve.wait_ge(pr_made, t - 1)
                src, m = split_heads(q)
                dst = diff[u][:, 4 * q:4 * q + 4, :].rearrange("p (b h) k -> p b h k", b=2)
                dve.tensor_tensor(dst, src, m.unsqueeze(3).to_broadcast([P, 2, 2, KEYS]),
                                  ALU.subtract).then_inc(diff_made, 1)

            def step(t, u, i, has):
                v = 1 - u
                if has(0):
                    maxima(t, 0)
                if has(-2):
                    dve.wait_ge(wo_psum, t - 1)
                    dve.wait_ge(xb_made, t - 1)
                    if not isinstance(t, int) or t >= 4:
                        dve.wait_ge(x1_stored[u], 16 * (i - 1))
                        dve.wait_ge(xn2_made, t - 3)
                    dve.tensor_tensor(x1[:, u, :], ps_c[:, 0:D], xb[:, u, :], ALU.add).then_inc(x1_made, 1)
                if has(0):
                    shift(t, u, 0)
                if has(-2):
                    dve.wait_ge(x1_made, t - 1)
                    dve.bn_stats(st2[:, u, :], x1[:, u, :]).then_inc(st2_made, 1)
                if has(0):
                    maxima(t, 1)
                if has(-2):
                    aggregate(t - 2, u, st2, st2_made, mv2, mv2_made)
                if has(0):
                    shift(t, u, 1)
                if has(-2):
                    add_eps(t - 2, u, mv2, mv2_made, var2_made)
                if has(2):
                    sums1(t + 2, u)
                if has(0):
                    maxima(t, 2)
                if has(-2):
                    norm2(t - 2, u, i - 1)
                if has(2):
                    aggregate(t + 2, u, st1, st1_made, mv1, mv1_made)
                if has(0):
                    shift(t, u, 2)
                if has(-1):
                    dve.wait_ge(fold_made, 5 * t)
                    dve.tensor_reduce(den[:, :], fold[:, v, :, :], AX.X, ALU.add).then_inc(den_made, 1)
                if has(2):
                    add_eps(t + 2, u, mv1, mv1_made, var1_made)
                if has(-1):
                    dve.wait_ge(den_made, t)
                    dve.reciprocal(rec[:, :], den[:, :]).then_inc(rec_made, 1)
                    dve.wait_ge(rec_made, t)
                    if not isinstance(t, int) or t >= 2:
                        dve.wait_ge(rT_psum, t - 1)
                    dve.tensor_copy(rden[:, :, :], rec[:, :].unsqueeze(2).to_broadcast([P, HEADS, DK]))\
                       .then_inc(rden_made, 1)
                if has(0):
                    maxima(t, 3)
                if has(2):
                    norm1(t + 2, u)
                if has(0):
                    shift(t, u, 3)
                if has(-1):
                    dve.wait_ge(rT_made, t)
                    if not isinstance(t, int) or t >= 3:
                        dve.wait_ge(wo_psum, t - 2)
                    dve.tensor_tensor(OT[:, v, :, :], ps_a[:, 0:D].rearrange("p (g n) -> p g n", g=GROUPS),
                                      rT[:, :, :], ALU.mult).then_inc(OT_made, 1)
                if has(-2):
                    dve.wait_ge(lg_psum, t - 1)
                    lt = LG[:, t - 2, :] if isinstance(t, int) else LG[:, bass.ds(t - 2, 1), :].squeeze(1)
                    dve.tensor_copy(lt, ps_c[:, 0:E]).then_inc(lg_made, 1)
            steps(dve, step)

            done = [0]

            def then(ins):
                done[0] += 1
                ins.then_inc(r_step, 1)
                dve.wait_ge(r_step, done[0])

            wide = [P, TILES, E]
            bc_t = lambda a: a.unsqueeze(2).to_broadcast(wide)
            bc_e = lambda a: a.unsqueeze(1).to_broadcast(wide)
            dve.wait_ge(lg_made, TILES)
            dve.wait_ge(ld_c, 80)
            then(dve.tensor_copy(before_bf[:, :], before_sb[:, :]))

            def top(src, m, o):
                then(dve.tensor_reduce(m, src, AX.X, ALU.max))
                then(dve.tensor_tensor(r_b[:, :, :], src, bc_t(m), ALU.is_ge))
                then(dve.tensor_tensor(r_b[:, :, :], r_b[:, :, :], bc_e(em8_sb[:, :]), ALU.mult))
                then(dve.tensor_reduce(r_c[:, :], r_b[:, :, :], AX.X, ALU.min))
                then(dve.tensor_tensor(o, bc_e(em8_sb[:, :]), bc_t(r_c[:, :]), ALU.is_equal))

            top(LG[:, :, :], r_m1[:, :], r_o1[:, :, :])
            dve.tensor_tensor(r_a[:, :, :], LG[:, :, :], bc_t(r_m1[:, :]), ALU.subtract).then_inc(r_shift, 1)
            then(dve.scalar_tensor_tensor(r_rank[:, 0:TILES, :], r_o1[:, :, :], -3e38, LG[:, :, :], ALU.mult, ALU.add))
            top(r_rank[:, 0:TILES, :], r_m2[:, :], r_o2[:, :, :])
            dve.tensor_tensor(r_s[:, :], r_m2[:, :], r_m1[:, :], ALU.subtract).then_inc(r_shift, 1)
            then(dve.memset(r_pick[:, TILES, :], 0.0))
            dve.tensor_tensor(r_pick[:, 0:TILES, :], r_o1[:, :, :], r_o2[:, :, :], ALU.add).then_inc(pick_made, 1)
            dve.wait_ge(r_exp, 2)
            then(dve.tensor_reduce(r_c[:, :], r_ex[:, :, :], AX.X, ALU.add))
            then(dve.reciprocal(XR[:, :, D + 1], r_c[:, :]))
            then(dve.tensor_tensor(XR[:, :, D + 2], r_e2[:, :], XR[:, :, D + 1], ALU.mult))
            dve.wait_ge(rank_psum, 1)
            then(dve.tensor_copy(r_rank[:, :, :], ps_a[:, 0:(TILES + 1) * E].rearrange("p (t e) -> p t e", e=E)))
            then(dve.tensor_scalar(r_i[:, :], r_rank[:, TILES, :], float(P - 1), None, ALU.add))
            then(dve.tensor_scalar(r_i2[:, :], r_i[:, :], 7, None, ALU.logical_shift_right))
            then(dve.tensor_scalar(r_n[:, :], r_i2[:, :], 1.0, None, ALU.max))
            then(dve.memset(r_p[:, :, :], 0.0))
            then(dve.tensor_copy(r_p[:, 0, 4:4 + E], r_n[:, :]))
            for n, d in enumerate((1, 2, 4)):
                then(dve.tensor_tensor(r_p[:, 1 - n % 2, 4:4 + E], r_p[:, n % 2, 4:4 + E],
                                       r_p[:, n % 2, 4 - d:4 + E - d], ALU.add))
            then(dve.tensor_tensor(r_st[:, :], r_p[:, 1, 4:4 + E], r_n[:, :], ALU.subtract))
            then(dve.tensor_scalar(r_base[:, :], r_st[:, :], float(P), None, ALU.mult))
            then(dve.tensor_tensor(r_a[:, :, :], r_rank[:, 0:TILES, :], bc_e(r_base[:, :]), ALU.add))
            for k, o in ((0, r_o1), (1, r_o2)):
                then(dve.tensor_tensor(r_b[:, :, :], r_a[:, :, :], o[:, :, :], ALU.mult))
                then(dve.tensor_reduce(r_pos[:, k, :], r_b[:, :, :], AX.X, ALU.add))
            then(dve.tensor_copy(XR[:, :, D + 3], r_pos[:, 0, :]))
            dve.tensor_copy(pos_i[:, :, :], r_pos[:, :, :]).then_inc(rows_made, 1)
            then(dve.tensor_tensor(t_cmp[:, :, :], slotno_sb[:, :].unsqueeze(2).to_broadcast([1, SLOTS, E]),
                                   r_st[0:1, :].unsqueeze(1).to_broadcast([1, SLOTS, E]), ALU.is_ge))
            then(dve.tensor_reduce(t_e[:, :], t_cmp[:, :, :], AX.X, ALU.add))
            then(dve.tensor_scalar(t_ei[:, :], t_e[:, :], -1.0, None, ALU.add))
            then(dve.memset(t_first[:, 0:1], 0.0))
            then(dve.tensor_tensor(t_first[:, 1:SLOTS], t_e[:, 1:SLOTS], t_e[:, 0:SLOTS - 1], ALU.subtract))
            then(dve.scalar_tensor_tensor(t_first[:, :], t_e[:, :], float(E) - 0.5, t_first[:, :],
                                          ALU.is_lt, ALU.mult))
            then(dve.tensor_tensor(t_first[:, :], t_first[:, :], t_e[:, :], ALU.mult))
            dve.tensor_copy(t_next[:, :], t_first[:, :]).then_inc(tables_made, 1)

            def split_weights(e, par, n):
                dve.wait_ge(w_hi, HALVES * e + n + 1)
                at = (slice(None), par) if isinstance(par, int) else (slice(None), bass.ds(par, 1))
                hi, lo = (WS[at + (k, slice(n * WH, (n + 1) * WH))] for k in range(2))
                if not isinstance(par, int):
                    hi, lo = hi.squeeze(1), lo.squeeze(1)
                dve.tensor_tensor(lo, wraw[:, n * WH:(n + 1) * WH], hi.bitcast(fp32),
                                  ALU.subtract).then_inc(w_lo, 1)
            for e in range(2):
                for n in range(HALVES):
                    split_weights(e, e, n)

            def take_rows(s, u):
                dve.wait_ge(xgT_psum, s + 1)
                if not isinstance(s, int) or s >= 2:
                    dve.wait_ge(up_psum, s - 1)
                rows = ps_c[:, 0:D].rearrange("p (c n) -> p c n", c=KC)
                dve.tensor_copy(xgT[:, u % 2, 0, :, :], rows).then_inc(xgT_hi, 1)
                dve.wait_ge(xgT_hi, s + 1)
                dve.tensor_tensor(xgT[:, u % 2, 1, :, :], rows, xgT[:, u % 2, 0, :, :].bitcast(fp32),
                                  ALU.subtract).then_inc(xgT_made, 1)
                sl = slots_sb[:, s:s + 1] if isinstance(s, int) else slots_sb[:, bass.ds(s, 1)]
                if not isinstance(s, int) or s >= 4:
                    dve.wait_ge(added, 16 * (s - 3))
                dve.tensor_copy(rowtok[:, u:u + 1], XG[:, u, D:D + 1].bitcast(i32))
                dve.tensor_tensor(wrow[:, u, 0:1], XG[:, u, D + 3:D + 4], sl, ALU.is_equal).then_inc(wr1, 1)
                dve.wait_ge(wr1, s + 1)
                dve.tensor_scalar(wrow[:, u, 1:2], wrow[:, u, 0:1], -1.0, 1.0, ALU.mult, ALU.add).then_inc(wr2, 1)
                dve.wait_ge(wr2, s + 1)
                dve.tensor_tensor(wrow[:, u, 2:3], wrow[:, u, 1:2], XG[:, u, D + 2:D + 3], ALU.mult).then_inc(wr3, 1)
                dve.wait_ge(wr3, s + 1)
                dve.scalar_tensor_tensor(wrow[:, u, 3:4], wrow[:, u, 0:1], XG[:, u, D + 1:D + 2], wrow[:, u, 2:3],
                                         ALU.mult, ALU.add).then_inc(wrow_made, 1)
            take_rows(0, 0)
            take_rows(1, 1)

            def slot(s, u, i, has):
                if has(1) and s_after_first(s):
                    to_split = dve.value_load(table(t_next, s), min_val=0, max_val=E - 1)
                for a in range(2):
                    dve.wait_ge(hidT_hi, 2 * s + a + 1)
                    dve.tensor_tensor(hidT[:, 1, 4 * a:4 * a + 4, :], ps_t[a][:, :].rearrange("p (a n) -> p a n", a=4),
                                      hidT[:, 0, 4 * a:4 * a + 4, :].bitcast(fp32), ALU.subtract).then_inc(hidT_lo, 1)
                if has(2):
                    take_rows(s + 2, (u + 2) % 4)
                if has(1) and s_after_first(s):
                    with dve.If(to_split > 0):
                        split_weights(to_split, to_split % 2, 0)
                dve.wait_ge(down_psum, s + 1)
                dve.wait_ge(wrow_made, s + 1)
                if not isinstance(s, int) or s >= 2:
                    dve.wait_ge(added, 16 * (s - 1))
                dve.tensor_scalar(ys[:, u % 2, :], ps_s[1][:, u % 2, 0:D], wrow[:, u, 3:4], None,
                                  ALU.mult).then_inc(ys_made, 1)
                if has(1) and s_after_first(s):
                    with dve.If(to_split > 0):
                        split_weights(to_split, to_split % 2, 1)
            ff_slots(dve, slot)

        @block.tensor
        def _(pe):
            mm = pe.matmul
            pe.wait_ge(ld_ctx, 96)
            for g in range(GROUPS):
                for c in range(KC):
                    last = mm(ps_s[0][:, g, 0:B * KEYS], wk_sb[:, c, g * P:(g + 1) * P], ctx_sb[:, c, :],
                              start=c == 0, stop=c == KC - 1)
            last.then_inc(k_psum, 1)
            for b in range(B):
                for c in range(KC):
                    mm(ps_s[1][:, b, 0:D], ctx_sb[:, c, b * KEYS:b * KEYS + P], wv_sb[:, c, :],
                       start=c == 0, stop=c == KC - 1)
                for j in range(4):
                    for c in range(KC):
                        last = mm(ps_s[1][32 * j:32 * j + REM, b, D:2 * D],
                                  ctx_sb[:, c, b * KEYS + P:(b + 1) * KEYS], wv_sb[:, c, :],
                                  start=c == 0, stop=c == KC - 1)
            last.then_inc(v_psum, 1)

            def xn_transposes(t, u):
                pe.wait_ge(xn_made, t + 1)
                if not isinstance(t, int) or t >= 3:
                    pe.wait_ge(OT_made, t - 2)
                for c in range(KC):
                    last = pe.transpose(ps_a[:, c * P:(c + 1) * P], xn[:, u, c * P:(c + 1) * P], id_sb[:, :])
                last.then_inc(xnT_psum, 1)

            def q_product(t, u):
                pe.wait_ge(xnT_made, t + 1)
                for g in range(GROUPS):
                    for c in range(KC):
                        last = mm(ps_a[:, D + g * P:D + (g + 1) * P], wq_sb[:, c, g * P:(g + 1) * P],
                                  xnT[:, u, c, :], start=c == 0, stop=c == KC - 1)
                last.then_inc(q_psum, 1)

            pe.wait_ge(ld_w, 96)
            xn_transposes(0, 0)
            q_product(0, 0)
            pe.wait_ge(kb_made, B * GROUPS * 2)
            pe.wait_ge(v_made, B * 6)

            def scores(t, u, q):
                n = 4 * t + q
                if q == 0:
                    pe.wait_ge(q_split, t + 1)
                if q >= 2 or not isinstance(t, int) or t >= 1:
                    pe.wait_ge(diff_made, n - 1)
                g, j0 = q // 2, 4 * (q % 2)
                for j in range(2):
                    for k, (a, kb) in enumerate(((q_hi, kb_hi), (q_hi, kb_lo), (q_lo, kb_hi))):
                        if isinstance(t, int):
                            rhs = kb[:, t // (TILES // B), g, j0 + 2 * j:j0 + 2 * j + 2, :]
                        else:
                            rhs = kb[:, bass.ds(t // (TILES // B), 1), g, j0 + 2 * j:j0 + 2 * j + 2, :].squeeze(1)
                        last = mm(ps_s[q % 2][:, j, 0:2 * KEYS].rearrange("p (h k) -> p h k", h=2),
                                  a[:, u, g, :], rhs, start=k == 0, stop=k == 2)
                last.then_inc(s_psum, 1)

            def p_transposes(t, k, u):
                if not isinstance(t, int) or 5 * t + k >= 2:
                    pe.wait_ge(t_made, 5 * t + k - 1)
                if k < 4:
                    pe.wait_ge(p_made, 4 * t + k + 1)
                else:
                    pe.wait_ge(pr_made, t + 1)
                for j in range(4):
                    src = pm[u][:, 4 * k + j, :] if k < 4 else \
                        pr[:, u, 4 * j:4 * j + 4, :].rearrange("p h k -> p (h k)")
                    last = pe.transpose(ps_t[(5 * u + k) % 2][:, j * P:(j + 1) * P], src, id_sb[:, :])
                last.then_inc(t_psum, 1)

            def pv(t, u, i):
                pe.wait_ge(t_made, 5 * t + 5)
                pe.wait_ge(vcur_made[u], 16 * i + 16)
                if not isinstance(t, int) or t < TILES - 2:
                    pe.wait_ge(qf_made, t + 3)
                for g in range(GROUPS):
                    cols = slice(g * P, (g + 1) * P)
                    for a in range(2):
                        qd = 2 * g + a
                        mm(ps_a[64 * a:64 * a + 64, cols], V_cur[:, u, HEADS * 32 + 64 * qd:HEADS * 32 + 64 * qd + 64],
                           PT[:, 4, qd, :], start=True, stop=True, skip_group_check=True)
                    for a in range(2):
                        for r in range(4):
                            h = g * GH + 2 * r + a
                            last = mm(ps_a[32 * r:32 * r + 32, cols], V_cur[:, u, 32 * h:32 * h + 32],
                                      PT[:, h // 4, h % 4, :], start=False, stop=True, skip_group_check=True)
                last.then_inc(pv_psum, 1)

            def rec_transposes(t):
                pe.wait_ge(rden_made, t + 1)
                for g in range(GROUPS):
                    last = pe.transpose(ps_a[:, D + g * P:D + (g + 1) * P],
                                        rden[:, g * GH:(g + 1) * GH, :].rearrange("p h c -> p (h c)"), id_sb[:, :])
                last.then_inc(rT_psum, 1)

            def wo_product(t, u):
                pe.wait_ge(OT_made, t + 1)
                if not isinstance(t, int) or t >= 1:
                    pe.wait_ge(lg_made, t)
                for g in range(GROUPS):
                    last = mm(ps_c[:, 0:D], OT[:, u, g, :], wo_sb[:, g, :], start=g == 0, stop=g == GROUPS - 1)
                last.then_inc(wo_psum, 1)

            def xn2_transposes(t, u):
                pe.wait_ge(xn2_made, t + 1)
                for c in range(KC):
                    last = pe.transpose(ps_c[:, c * P:(c + 1) * P], xn2[:, u, c * P:(c + 1) * P], id_sb[:, :])
                last.then_inc(xn2T_psum, 1)

            def router(t, u):
                pe.wait_ge(xn2T_made, t + 1)
                for c in range(KC):
                    last = mm(ps_c[:, 0:E], xn2T[:, c, :], rw_sb[:, c, :], start=c == 0, stop=c == KC - 1)
                last.then_inc(lg_psum, 1)

            def step(t, u, i, has):
                v = 1 - u
                if has(0):
                    scores(t, u, 1)
                if has(-2):
                    wo_product(t - 2, u)
                if has(-1):
                    p_transposes(t - 1, 2, v)
                if has(1):
                    xn_transposes(t + 1, v)
                if has(-1):
                    p_transposes(t - 1, 3, v)
                if has(0):
                    scores(t, u, 2)
                if has(-1):
                    p_transposes(t - 1, 4, v)
                if has(1):
                    q_product(t + 1, v)
                if has(0):
                    scores(t, u, 3)
                if has(-1):
                    pv(t - 1, v, i if v == 0 else i - 1)
                if has(-2):
                    xn2_transposes(t - 2, u)
                if has(1):
                    scores(t + 1, v, 0)
                if has(-1):
                    rec_transposes(t - 1)
                if has(0):
                    p_transposes(t, 0, u)
                if has(-2):
                    router(t - 2, u)
                if has(0):
                    p_transposes(t, 1, u)
            scores(0, 0, 0)
            steps(pe, step)

            pe.wait_ge(pick_made, 1)
            pe.wait_ge(const_made, 3)
            cols = ps_a[:, 0:(TILES + 1) * E].rearrange("p (t e) -> p t e", e=E)
            mm(cols, before_bf[:, :], r_pick[:, :, :], start=True, stop=True)
            for t in range(TILES):
                last = mm(cols[:, t + 1:TILES + 1, :], ones_bf[:, :],
                          r_pick[:, t:t + 1, :].to_broadcast([P, TILES - t, E]),
                          start=False, stop=True, skip_group_check=True)
            last.then_inc(rank_psum, 1)

            def row_transposes(s, u):
                count = s // 4 + 1
                pe.wait_ge(xg_loaded[u], 16 * count)
                if not isinstance(s, int) or s >= 1:
                    pe.wait_ge(xgT_made, s)
                for c in range(KC):
                    last = pe.transpose(ps_c[:, c * P:(c + 1) * P], XG[:, u, c * P:(c + 1) * P], id_sb[:, :])
                last.then_inc(xgT_psum, 1)

            w1 = WS[:, :, :, 0:KC * HID].rearrange("p e s (c h) -> p e s c h", c=KC)
            w2 = WS[:, :, :, KC * HID:WB].rearrange("p e s (j d) -> p e s j d", j=HJ)
            PARTS = ((0, 0), (0, 1), (1, 0))

            def up(s, u, e):
                par = e % 2
                pe.wait_ge(w_hi, HALVES * e + HALVES)
                pe.wait_ge(w_lo, HALVES * e + HALVES)
                pe.wait_ge(xgT_made, s + 1)
                if not isinstance(s, int) or s >= 1:
                    pe.wait_ge(hid_made, s)
                for c in range(2):
                    for k in range(KC):
                        for n, (a, w) in enumerate(PARTS):
                            last = mm(ps_s[0][:, c, :], xgT[:, u % 2, a, k, :],
                                      w1[:, bass.ds(par, 1), w, k, 512 * c:512 * (c + 1)].squeeze(1),
                                      start=k == 0 and n == 0, stop=k == KC - 1 and n == 2)
                last.then_inc(up_psum, 1)

            def expert(s):
                return pe.value_load(table(t_ei, s), min_val=0, max_val=E - 1)

            def down(s, u, e):
                par = e % 2
                pe.wait_ge(hidT_lo, 2 * s + 2)
                if not isinstance(s, int) or s >= 2:
                    pe.wait_ge(ys_made, s - 1)
                for j in range(HJ):
                    for n, (a, w) in enumerate(PARTS):
                        last = mm(ps_s[1][:, u % 2, 0:D], hidT[:, a, j, :],
                                  w2[:, bass.ds(par, 1), w, j, :].squeeze(1),
                                  start=j == 0 and n == 0, stop=j == HJ - 1 and n == 2)
                last.then_inc(down_psum, 1)

            row_transposes(0, 0)
            row_transposes(1, 1)
            pe.wait_ge(tables_made, 1)
            up(0, 0, expert(0))

            def slot(s, u, i, has):
                e0 = expert(s)
                if has(1):
                    e1 = expert(s + 1)
                pe.wait_ge(hid_made, s + 1)
                for j in range(HJ):
                    last = pe.transpose(ps_t[j // 4][:, (j % 4) * P:(j % 4 + 1) * P], hid[:, j * P:(j + 1) * P],
                                        id_sb[:, :])
                last.then_inc(hidT_psum, 1)
                if has(2):
                    row_transposes(s + 2, (u + 2) % 4)
                if has(1):
                    up(s + 1, (u + 1) % 4, e1)
                down(s, u, e0)
            ff_slots(pe, slot)


def kernel(x, ctx_1024, L0_xattn_Wq, L0_xattn_bq, L0_xattn_Wk, L0_xattn_bk, L0_xattn_Wv, L0_xattn_bv,
           L0_xattn_Wo, L0_xattn_bo, L0_ffn_router_w, L0_ffn_w1, L0_ffn_w2):
    import concourse.bacc as _bacc
    from concourse.bass_utils import run_bass_kernel_spmd as _run

    def laid(a, *order):
        return np.ascontiguousarray(np.asarray(a).transpose(*order)) if order else np.asarray(a)

    w1 = laid(L0_ffn_w1, 0, 2, 1).reshape(E, KC, P, HID).transpose(0, 2, 1, 3).reshape(E, P, KC * HID)
    w2 = laid(L0_ffn_w2, 0, 2, 1).reshape(E, HJ, P, D).transpose(0, 2, 1, 3).reshape(E, P, HJ * D)
    lanes = np.arange(P)
    data = {
        "x": laid(x).reshape(TOK, D),
        "ctxT": laid(ctx_1024, 2, 0, 1).reshape(D, B * KEYS),
        "wq": laid(L0_xattn_Wq, 1, 0, 2).reshape(D, D),
        "bq": laid(L0_xattn_bq).reshape(D),
        "wk": laid(L0_xattn_Wk, 1, 0, 2).reshape(D, D),
        "bk": laid(L0_xattn_bk).reshape(D),
        "wv": laid(L0_xattn_Wv, 1, 0, 2).reshape(D, D),
        "bv": laid(L0_xattn_bv).reshape(D),
        "wo": laid(L0_xattn_Wo),
        "bo": laid(L0_xattn_bo),
        "rwT": laid(L0_ffn_router_w, 1, 0),
        "wexp": np.concatenate([w1, w2], axis=2),
        "ident": np.eye(P, dtype=np.float32),
        "headmask": (lanes[:, None] // DK == np.arange(GH)[None]).astype(np.float32),
        "before": (lanes[:, None] < lanes[None]).astype(np.float32),
        "em8": np.broadcast_to(np.arange(E) - float(E), (P, E)).astype(np.float32),
        "tokid": (np.arange(TILES + 1)[None] * P + lanes[:, None]).astype(np.int32),
        "slots": np.concatenate([np.arange(SLOTS)[None] * P + lanes[:, None],
                                 np.arange(SLOTS)[None]]).astype(np.float32),
    }
    nc = _bacc.Bacc("TRN2", target_bir_lowering=False, num_devices=1)
    arrays, args = {}, []
    for name, a in data.items():
        arrays[f"in_{name}"] = np.ascontiguousarray(a)
        args.append(nc.dram_tensor(f"in_{name}", a.shape, mybir.dt.from_np(a.dtype), kind="ExternalInput").ap())
    args.append(nc.dram_tensor("result", [TOK + P, D], mybir.dt.float32, kind="ExternalOutput").ap())
    xattn_moe_kernel(nc, *args)
    r = _run(nc, [arrays], core_ids=[0])
    return r.results[0]["result"][0:TOK].reshape(B, S, D)
```

```python
import numpy as np
import concourse.bass as bass
from concourse import mybir
from contextlib import ExitStack, nullcontext

B, S, D = 2, 1024, 256
KEYS = 154
HEADS, DK = 16, 16
E, HID = 8, 1024
TOK = B * S
P = 128
TILES = TOK // P
KC = D // P
REM = KEYS - P
GH = P // DK
GROUPS = HEADS // GH
QUADS = HEADS // 4
SLOTS = (2 * TOK + E * (P - 1)) // P
ROW = D + 2
PICKS = 2 * TILES
HJ = HID // P
WB = KC * HID + HJ * D
VW = HEADS * 32 + QUADS * 64
EPS = 1e-5


def xattn_moe_kernel(nc, x, ctxT, wq, bq, wk, bk, wv, bv, wo, bo, rwT, wexp,
                     ident, headmask, before, em8, count, tilecode, lane, out):
    fp32, f32r = mybir.dt.float32, mybir.dt.float32r
    bf16, i32 = mybir.dt.bfloat16, mybir.dt.int32
    ALU, ACT, AX = mybir.AluOpType, mybir.ActivationFunctionType, mybir.AxisListType

    rows = nc.dram_tensor("rows", [TOK + P, ROW], fp32).ap()

    with ExitStack() as ctx:
        def sb(name, shape, dt=fp32):
            return ctx.enter_context(nc.sbuf_tensor(name, shape, dt))

        def sem(name):
            return ctx.enter_context(nc.semaphore(name))

        id_sb = sb("id_sb", [P, P])
        mask_sb = sb("mask_sb", [P, GH])
        before_sb = sb("before_sb", [P, P])
        before_bf = sb("before_bf", [P, P], bf16)
        ones_bf = sb("ones_bf", [P, P], bf16)
        em8_sb = sb("em8_sb", [P, E])
        count_sb = sb("count_sb", [P, P])
        tilecode_sb = sb("tilecode_sb", [P, PICKS])
        lane_sb = sb("lane_sb", [P, 1])
        wq_sb = sb("wq_sb", [P, KC, D])
        wo_sb = sb("wo_sb", [P, KC, D])
        rw_sb = sb("rw_sb", [P, KC, E])
        bq_sb = sb("bq_sb", [P, GROUPS])
        bq4_sb = sb("bq4_sb", [P, GROUPS])
        bk_sb = sb("bk_sb", [P, GROUPS])
        bv_sb = sb("bv_sb", [P, D])
        bo_sb = sb("bo_sb", [P, D])
        half_sb = sb("half_sb", [P, 1])
        xs = sb("xs", [P, TILES, D])
        LG = sb("LG", [P, TILES, E])
        KBN = B * GROUPS * GH * KEYS
        KB = sb("KB", [P, 2 * 2 * WB], f32r)
        WS = KB[:, :].rearrange("p (e s w) -> p e s w", e=2, s=2)
        kb_hi = KB[:, 0:KBN].rearrange("p (b g j k) -> p b g j k", b=B, g=GROUPS, j=GH)
        kb_lo = KB[:, KBN:2 * KBN].rearrange("p (b g j k) -> p b g j k", b=B, g=GROUPS, j=GH)
        V_all = sb("V_all", [P, B, VW])
        V_cur = sb("V_cur", [P, 2, VW])
        big = sb("big", [P, 2 * (HEADS * KEYS + HEADS * P)])
        DSZ = HEADS * KEYS
        diff = [big[:, u * DSZ:(u + 1) * DSZ].rearrange("p (h k) -> p h k", h=HEADS) for u in range(2)]
        o1 = 2 * DSZ
        pm = [big[:, o1 + u * HEADS * P:o1 + (u + 1) * HEADS * P].rearrange("p (h k) -> p h k", h=HEADS)
              for u in range(2)]
        o2 = o1 + 2 * HEADS * P
        ctx_sb = big[:, 0:KC * B * KEYS].rearrange("p (c n) -> p c n", c=KC)
        wk_sb = big[:, 1024:1024 + KC * D].rearrange("p (c n) -> p c n", c=KC)
        wv_sb = big[:, 2048:2048 + KC * D].rearrange("p (c n) -> p c n", c=KC)
        KT = big[:, 3072:3072 + GROUPS * B * KEYS].rearrange("p (g n) -> p g n", g=GROUPS)
        o3 = 2 * KBN
        KTr = KB[:, o3:o3 + 2 * GROUPS * B * KEYS].rearrange("p (s g n) -> p s g n", s=2, g=GROUPS)
        wraw = big[:, 0:WB]
        pr = sb("pr", [P, 2, HEADS, 32])
        PT = sb("PT", [P, 5, 4, P])
        half = sb("half", [P, 4, 64])
        fold = sb("fold", [P, 2, HEADS, 32])
        st1 = sb("st1", [P, 2, 6])
        mv1 = sb("mv1", [P, 2, 4])
        xn = sb("xn", [P, 2, D])
        xnT = sb("xnT", [P, 2, KC, P])
        qf = sb("qf", [P, 2, GROUPS, P])
        o4 = o3 + 2 * GROUPS * B * KEYS
        q_hi = KB[:, o4:o4 + 2 * D].rearrange("p (u g n) -> p u g n", u=2, g=GROUPS)
        q_lo = KB[:, o4 + 2 * D:o4 + 4 * D].rearrange("p (u g n) -> p u g n", u=2, g=GROUPS)
        mx = sb("mx", [P, 2, 4])
        den = sb("den", [P, HEADS])
        rec = sb("rec", [P, HEADS])
        rden = sb("rden", [P, HEADS, DK])
        rT = sb("rT", [P, GROUPS, P])
        OT = sb("OT", [P, 2, GROUPS, P])
        xb = sb("xb", [P, 2, D])
        x1 = sb("x1", [P, 2, D])
        st2 = sb("st2", [P, 2, 6])
        mv2 = sb("mv2", [P, 2, 4])
        xn2 = sb("xn2", [P, 2, D])
        xn2T = sb("xn2T", [P, KC, P])
        zero = sb("zero", [P, ROW])
        wts = sb("wts", [P, TILES, 2])
        r_a, r_b = (half[:, 2 * u:2 * u + 2, :].rearrange("p a (t e) -> p (a t) e", e=E) for u in range(2))
        r_o1, r_o2, r_ex = (fold[:, 0, 4 * n:4 * n + 4, :].rearrange("p a (t e) -> p (a t) e", e=E)
                            for n in range(3))
        r_m1 = sb("r_m1", [P, TILES])
        r_m2 = sb("r_m2", [P, TILES])
        r_c = sb("r_c", [P, TILES])
        r_e2 = sb("r_e2", [P, TILES])
        r_s = sb("r_s", [P, TILES])
        r_pick = sb("r_pick", [P, TILES + 1, E], bf16)
        r_rank = sb("r_rank", [P, TILES + 1, E])
        r_i = sb("r_i", [P, E], i32)
        r_i2 = sb("r_i2", [P, E], i32)
        r_n = sb("r_n", [P, E])
        r_p = sb("r_p", [P, 2, 4 + E])
        r_st = sb("r_st", [P, E])
        r_base = sb("r_base", [P, E])
        r_pos = sb("r_pos", [P, 2, TILES])
        pos_i = sb("pos_i", [P, PICKS], i32)
        slot_i = sb("slot_i", [P, PICKS], i32)
        slot_f = sb("slot_f", [P, PICKS])
        lane_f = sb("lane_f", [P, PICKS])
        at_lane = sb("at_lane", [P, PICKS, P], bf16)
        at_slot = sb("at_slot", [P, PICKS, SLOTS], bf16)
        coded = sb("coded", [P, PICKS, 2, SLOTS], bf16)
        codes = sb("codes", [P, 2, SLOTS])
        t_k = sb("t_k", [P, 2, SLOTS])
        t_a = sb("t_a", [P, SLOTS])
        t_b = sb("t_b", [P, SLOTS])
        tok_i = sb("tok_i", [P, SLOTS], i32)
        t_cmp = sb("t_cmp", [1, SLOTS + 1, E])
        t_e = sb("t_e", [1, SLOTS + 1])
        t_sum = sb("t_sum", [1, SLOTS])
        t_pair = sb("t_pair", [1, SLOTS], i32)
        t_val = sb("t_val", [1, SLOTS])
        t_first = sb("t_first", [1, SLOTS + 3])
        t_short = sb("t_short", [1, SLOTS + 1])
        t_tmp = sb("t_tmp", [1, SLOTS])
        t_used = sb("t_used", [1, 1], i32)
        t_split = sb("t_split", [1, SLOTS], i32)
        XG = big[:, WB:WB + 4 * ROW].rearrange("p (u c) -> p u c", u=4)
        xgT = sb("xgT", [P, 2, 2, KC, P], f32r)
        wrow = sb("wrow", [P, 4, 4])
        gtok = sb("gtok", [P, 4], i32)
        rowtok = sb("rowtok", [P, 4], i32)
        hid = big[:, WB + 4 * ROW:WB + 4 * ROW + HID]
        hidT = sb("hidT", [P, 2, HJ, P], f32r)
        o5 = WB + 4 * ROW + HID
        ys = big[:, o5:o5 + 2 * D].rearrange("p (u d) -> p u d", u=2)

        ps_s = [ctx.enter_context(nc.psum_tensor(f"ps_s{u}", [P, 2, 512], fp32)) for u in range(2)]
        ps_t = [ctx.enter_context(nc.psum_tensor(f"ps_t{u}", [P, 512], fp32)) for u in range(2)]
        ps_a = ctx.enter_context(nc.psum_tensor("ps_a", [P, 512], fp32))
        ps_c = ctx.enter_context(nc.psum_tensor("ps_c", [P, 512], fp32))

        ld_k, ld_v, ld_q, ld_w, ld_c, ld_x0, ld_x1 = (sem(n) for n in
            ("ld_k", "ld_v", "ld_q", "ld_w", "ld_c", "ld_x0", "ld_x1"))
        zero_made, zero_stored, wts_made, wts_stored = (sem(n) for n in ("zero_made", "zero_stored", "wts_made", "wts_stored"))
        const_made, v_zeroed, p_zeroed = sem("const_made"), sem("v_zeroed"), sem("p_zeroed")
        bq_made = sem("bq_made")
        k_psum, k_made, kt_hi, kt_lo, kb_made, kb1_made = (sem(n) for n in
            ("k_psum", "k_made", "kt_hi", "kt_lo", "kb_made", "kb1_made"))
        kg1_made = sem("kg1_made")
        v_psum, v_made = sem("v_psum"), sem("v_made")
        st1_made, mv1_made, var1_made, rstd1_made = (sem(n) for n in ("st1_made", "mv1_made", "var1_made", "rstd1_made"))
        xn_made, xnT_psum, xnT_made = sem("xn_made"), sem("xnT_psum"), sem("xnT_made")
        q_psum, qf_made, q_hi_made, q_split = sem("q_psum"), sem("qf_made"), sem("q_hi_made"), sem("q_split")
        s_psum, mx_made, diff_made, p_made, pr_made = (sem(n) for n in ("s_psum", "mx_made", "diff_made", "p_made", "pr_made"))
        t_psum, t_made = sem("t_psum"), sem("t_made")
        half_made, fold_made, den_made, rec_made, rden_made = (sem(n) for n in
            ("half_made", "fold_made", "den_made", "rec_made", "rden_made"))
        pv_psum, rT_psum, rT_made, OT_made = (sem(n) for n in ("pv_psum", "rT_psum", "rT_made", "OT_made"))
        xb_made, wo_psum, x1_made = sem("xb_made"), sem("wo_psum"), sem("x1_made")
        vcur_made = [sem(f"vcur_made{u}") for u in range(2)]
        x1_stored = [sem(f"x1_stored{u}") for u in range(2)]
        xr_stored = [sem(f"xr_stored{u}") for u in range(2)]
        st2_made, mv2_made, var2_made, rstd2_made, xn2_made = (sem(n) for n in ("st2_made", "mv2_made", "var2_made", "rstd2_made", "xn2_made"))
        xn2T_psum, xn2T_made, lg_psum, lg_made = (sem(n) for n in ("xn2T_psum", "xn2T_made", "lg_psum", "lg_made"))
        r_step, r_shift, r_exp, pick_made, rank_psum = (sem(n) for n in ("r_step", "r_shift", "r_exp", "pick_made", "rank_psum"))
        at_slot_made, at_lane_made, coded_made, codes_psum, toks_made, tables_made = (sem(n) for n in
            ("at_slot_made", "at_lane_made", "coded_made", "codes_psum", "toks_made", "tables_made"))
        w_loaded, w_hi, w_lo = sem("w_loaded"), sem("w_hi"), sem("w_lo")
        xg_loaded = [sem(f"xg_loaded{u}") for u in range(4)]
        xgT_psum, xgT_made, gtok_made, wr1, wrow_made = (sem(n) for n in
            ("xgT_psum", "xgT_made", "gtok_made", "wr1", "wrow_made"))
        up_psum, hid_made, hidT_psum, hidT_hi, hidT_lo, xgT_hi = (sem(n) for n in
            ("up_psum", "hid_made", "hidT_psum", "hidT_hi", "hidT_lo", "xgT_hi"))
        down_psum, ys_made, added = sem("down_psum"), sem("ys_made"), sem("added")

        dve_passed, pool_passed = sem("dve_passed"), sem("pool_passed")

        block = ctx.enter_context(nc.Block())

        LOOP0, LOOP1 = 4, TILES - 2

        def steps(eng, step):
            for t in range(LOOP0):
                step(t, t % 2, t // 2, lambda d, t=t: 0 <= t + d < TILES)
            with eng.Fori(LOOP0 // 2, LOOP1 // 2) as i:
                for u in range(2):
                    step(2 * i + u, u, i, lambda d: True)
            for t in range(LOOP1, TILES + 2):
                step(t, t % 2, t // 2, lambda d, t=t: 0 <= t + d < TILES)

        HALVES = 2
        WH = WB // HALVES
        FF_LOOP = 2 * TOK // P

        def ff_slots(eng, slot):
            for s in range(4):
                slot(s, s, 0, lambda d: True)
            with eng.Fori(1, FF_LOOP // 4) as i:
                for u in range(4):
                    slot(4 * i + u, u, i, lambda d: True)
            for s in range(FF_LOOP, SLOTS):
                with if_used(eng, s):
                    slot(s, s % 4, s // 4, lambda d, s=s: s + d < SLOTS)

        def block_keys(eng, b, g, made, parts=(0, 1)):
            for part in parts:
                kb = (kb_hi, kb_lo)[part]
                src = KTr[:, part, g, b * KEYS:(b + 1) * KEYS].bitcast(fp32)
                eng.tensor_tensor(kb[:, b, g, :, :], src.unsqueeze(1).to_broadcast([P, GH, KEYS]),
                                  mask_sb[:, :].unsqueeze(2).to_broadcast([P, GH, KEYS]), ALU.mult).then_inc(made, 1)

        def table(t, s):
            return t[0:1, s:s + 1] if isinstance(s, int) else t[0:1, bass.ds(s, 1)]

        def if_used(eng, s):
            if not isinstance(s, int) or s < FF_LOOP:
                return nullcontext()
            return eng.If(used[eng] > s)

        used = {}

        def read_used(eng):
            used[eng] = eng.value_load(t_used[0:1, 0:1], min_val=FF_LOOP, max_val=SLOTS)

        @block.sync
        def _(sp):
            sp.dma_start(ctx_sb, ctxT.rearrange("(c p) n -> p c n", p=P)).then_inc(ld_k, 16)
            sp.dma_start(wk_sb, wk.rearrange("(c p) n -> p c n", p=P)).then_inc(ld_k, 16)
            sp.dma_start(bk_sb[:, :], bk.rearrange("(g p) -> p g", p=P),
                         allow_slow_non_contiguous=True).then_inc(ld_k, 16)
            sp.dma_start(mask_sb[:, :], headmask).then_inc(ld_k, 16)
            sp.dma_start(wv_sb, wv.rearrange("(c p) n -> p c n", p=P)).then_inc(ld_v, 16)
            sp.dma_start(bv_sb[:, :], bv.unsqueeze(0).to_broadcast([P, D])).then_inc(ld_v, 16)
            sp.dma_start(before_sb[:, :], before).then_inc(ld_c, 16)
            sp.dma_start(em8_sb[:, :], em8).then_inc(ld_c, 16)
            sp.dma_start(count_sb[:, :], count).then_inc(ld_c, 16)
            sp.dma_start(tilecode_sb[:, :], tilecode).then_inc(ld_c, 16)
            sp.dma_start(lane_sb[:, :], lane).then_inc(ld_c, 16)
            sp.wait_ge(zero_made, 1)
            sp.dma_start(rows[TOK:TOK + P, :], zero[:, :]).then_inc(zero_stored, 16)
            sp.dma_start(out[TOK:TOK + P, :], zero[:, 0:D]).then_inc(zero_stored, 16)

            sp.wait_ge(v_made, B * 6)

            def step(t, u, i, has):
                if has(0):
                    if not isinstance(t, int) or t >= 2:
                        sp.wait_ge(pv_psum, t - 1)
                    src = V_all[:, t // (TILES // B), :] if isinstance(t, int) else \
                        V_all[:, bass.ds(t // (TILES // B), 1), :].squeeze(1)
                    sp.dma_start(V_cur[:, u, :], src).then_inc(vcur_made[u], 16)
                if has(-2):
                    sp.wait_ge(x1_made, t - 1)
                    sp.dma_start(out[bass.ds((t - 2) * P, P), :], x1[:, u, :]).then_inc(x1_stored[u], 16)
                    sp.wait_ge(xn2_made, t - 1)
                    sp.dma_start(rows[bass.ds((t - 2) * P, P), 0:D], xn2[:, u, :]).then_inc(xr_stored[u], 16)
            steps(sp, step)

            sp.wait_ge(t_psum, 5 * TILES)
            sp.wait_ge(fold_made, 5 * TILES)
            for e in range(E):
                if e == 1:
                    sp.wait_ge(wts_made, 1)
                    sp.dma_start(rows[0:TOK, D:D + 2].rearrange("(t p) c -> p t c", p=P), wts[:, :, :],
                                 allow_slow_non_contiguous=True).then_inc(wts_stored, 16)
                    for u in range(2):
                        sp.wait_ge(xg_loaded[u], 16)
                if e:
                    sp.wait_ge(w_lo, HALVES * e)
                sp.dma_start(wraw, wexp[e]).then_inc(w_loaded, 16)

        @block.gpsimd
        def _(pool):
            pool.memset(ones_bf[:, :], 1.0).then_inc(const_made, 1)
            pool.memset(half_sb[:, :], -0.5).then_inc(const_made, 1)
            pool.memset(zero[:, :], 0.0).then_inc(zero_made, 1)
            pool.memset(V_all[:, :, :], 0.0).then_inc(v_zeroed, 1)
            pool.memset(pr[:, :, :, :], 0.0).then_inc(p_zeroed, 1)
            pool.wait_ge(const_made, 2)

            def wait_alone(s, n):
                pool.wait_ge(s, n)
                if not isinstance(n, int):
                    pool.sem_inc(pool_passed, 1)

            def rstd(t, u, stats, made, rstd_made):
                pool.wait_ge(made, t + 1)
                pool.tensor_tensor(stats[:, u, 3:4], stats[:, u, 2:3], half_sb[:, :], ALU.pow).then_inc(rstd_made, 1)

            def xs_tile(t):
                return xs[:, bass.ds(t, 1), :].squeeze(1) if not isinstance(t, int) else xs[:, t, :]

            def split_q(t, u):
                pool.wait_ge(q_hi_made, t + 1)
                if not isinstance(t, int) or t >= 2:
                    wait_alone(s_psum, 4 * (t - 1))
                pool.tensor_tensor(q_lo[:, u, :, :], qf[:, u, :, :], q_hi[:, u, :, :].bitcast(fp32),
                                   ALU.subtract).then_inc(q_split, 1)

            def fold_quad(t, u, q):
                pool.wait_ge(p_made, 4 * t + q + 1)
                if q == 0 and (not isinstance(t, int) or t >= 2):
                    pool.wait_ge(den_made, t - 1)
                heads = slice(4 * q, 4 * q + 4)
                if q or not isinstance(t, int) or t >= 1:
                    pool.wait_ge(fold_made, 5 * t + q)
                pool.tensor_tensor(half[:, :, :], pm[u][:, heads, 0:64], pm[u][:, heads, 64:128],
                                   ALU.add).then_inc(half_made, 1)
                pool.wait_ge(half_made, 4 * t + q + 1)
                pool.tensor_tensor(fold[:, u, heads, :], half[:, :, 0:32], half[:, :, 32:64],
                                   ALU.add).then_inc(fold_made, 1)

            def fold_rest(t, u):
                pool.wait_ge(pr_made, t + 1)
                pool.wait_ge(fold_made, 5 * t + 4)
                pool.tensor_tensor(fold[:, u, :, :], fold[:, u, :, :], pr[:, u, :, :], ALU.add).then_inc(fold_made, 1)

            rstd(0, 0, mv1, var1_made, rstd1_made)
            rstd(1, 1, mv1, var1_made, rstd1_made)
            pool.wait_ge(ld_k, 64)
            pool.wait_ge(kt_lo, 1)
            block_keys(pool, 0, 1, kg1_made, (0,))
            split_q(0, 0)
            block_keys(pool, 0, 1, kg1_made, (1,))

            def step(t, u, i, has):
                v = 1 - u
                if isinstance(t, int) and t < GROUPS:
                    block_keys(pool, 1, t, kb1_made)
                if has(-1):
                    fold_quad(t - 1, v, 3)
                    fold_rest(t - 1, v)
                if has(-2):
                    rstd(t - 2, u, mv2, var2_made, rstd2_made)
                if has(0):
                    fold_quad(t, u, 0)
                if has(1):
                    split_q(t + 1, v)
                if has(0):
                    fold_quad(t, u, 1)
                if has(2):
                    rstd(t + 2, u, mv1, var1_made, rstd1_made)
                if has(-1):
                    if not isinstance(t, int) or t >= 3:
                        pool.wait_ge(x1_made, t - 2)
                    pool.tensor_tensor(xb[:, v, :], xs_tile(t - 1), bo_sb[:, :], ALU.add).then_inc(xb_made, 1)
                if has(0):
                    fold_quad(t, u, 2)

            pool.wait_ge(ld_w, 48)
            pool.wait_ge(ld_x1, 16)
            steps(pool, step)

            def split_first(n):
                pool.wait_ge(w_hi, n + 1)
                cols = slice(n * WH, (n + 1) * WH)
                pool.tensor_tensor(WS[:, 0, 1, cols], wraw[:, cols], WS[:, 0, 0, cols].bitcast(fp32),
                                   ALU.subtract).then_inc(w_lo, 1)
            split_first(0)
            pool.wait_ge(at_slot_made, 1)
            pool.tensor_tensor(coded[:, :, 1, :], at_slot[:, :, :],
                               tilecode_sb[:, :].unsqueeze(2).to_broadcast([P, PICKS, SLOTS]),
                               ALU.mult).then_inc(coded_made, 1)
            split_first(1)

            def gather(u):
                pool.indirect_dma_start(XG[:, u, :], None, rows,
                                        bass.IndirectOffsetOnAxis(gtok[:, u:u + 1], 0)).then_inc(xg_loaded[u], 16)
            pool.wait_ge(zero_stored, 32)
            for u in range(2):
                pool.wait_ge(xr_stored[u], 16 * TILES // 2)
            pool.wait_ge(wts_stored, 16)
            pool.wait_ge(gtok_made, 1)
            for u in range(4):
                gather(u)
            for u in range(2):
                pool.wait_ge(x1_stored[u], 16 * TILES // 2)

            def slot(s, u, i, has):
                if has(4):
                    wait_alone(gtok_made, s + 2)
                    wait_alone(xgT_made, s + 1)
                    wait_alone(wrow_made, s + 1)
                    gather(u)
                wait_alone(ys_made, s + 1)
                if not isinstance(s, int) or s >= 1:
                    wait_alone(added, 16 * s)
                pool.indirect_dma_start(out, bass.IndirectOffsetOnAxis(rowtok[:, u:u + 1], 0),
                                        ys[:, u % 2, :], None, compute_op=ALU.add).then_inc(added, 16)
                if isinstance(s, int) and s >= FF_LOOP:
                    pool.wait_ge(added, 16 * (s + 1))
            pool.wait_ge(tables_made, 1)
            read_used(pool)
            ff_slots(pool, slot)
            pool.wait_ge(added, 16 * FF_LOOP)

        @block.scalar
        def _(act):
            def to_cols(v, ap):
                return act.dma_start(ap, v.rearrange("(g p) -> p g", p=P), allow_slow_non_contiguous=True)
            xv = x.rearrange("(t p) d -> p t d", p=P)
            act.dma_start(xs[:, 0:2, :], xv[:, 0:2, :]).then_inc(ld_x0, 16)
            act.dma_start(id_sb[:, :], ident).then_inc(ld_q, 16)
            act.dma_start(wq_sb[:, :, :], wq.rearrange("(c p) n -> p c n", p=P)).then_inc(ld_q, 16)
            to_cols(bq, bq_sb[:, :]).then_inc(ld_q, 16)
            act.dma_start(xs[:, 2:4, :], xv[:, 2:4, :]).then_inc(ld_x0, 16)
            act.dma_start(bo_sb[:, :], bo.unsqueeze(0).to_broadcast([P, D])).then_inc(ld_w, 16)
            act.dma_start(wo_sb[:, :, :], wo.rearrange("(c p) n -> p c n", p=P)).then_inc(ld_w, 16)
            act.dma_start(rw_sb[:, :, :], rwT.rearrange("(c p) n -> p c n", p=P)).then_inc(ld_w, 16)
            act.dma_start(xs[:, 4:TILES, :], xv[:, 4:TILES, :]).then_inc(ld_x1, 16)
            act.wait_ge(ld_q, 48)
            act.mul(bq4_sb[:, :], bq_sb[:, :], DK ** -0.5).then_inc(bq_made, 1)
            act.wait_ge(bq_made, 1)

            def evac_xnT(t, u):
                act.wait_ge(xnT_psum, t + 1)
                if not isinstance(t, int) or t >= 2:
                    act.wait_ge(q_psum, t - 1)
                act.activation(xnT[:, u, :, :], ps_a[:, 0:KC * P].rearrange("p (c n) -> p c n", c=KC),
                               ACT.Copy).then_inc(xnT_made, 1)

            def evac_q(t, u):
                act.wait_ge(q_psum, t + 1)
                if not isinstance(t, int) or t >= 2:
                    act.wait_ge(q_split, t - 1)
                for g in range(GROUPS):
                    last = act.activation(qf[:, u, g, :], ps_a[:, D + g * P:D + (g + 1) * P], ACT.Identity,
                                          bias=bq4_sb[:, g:g + 1], scale=DK ** -0.5)
                last.then_inc(qf_made, 1)
                if not isinstance(t, int) or t >= 2:
                    act.wait_ge(s_psum, 4 * (t - 1))
                act.wait_ge(qf_made, t + 1)
                act.activation(q_hi[:, u, :, :], qf[:, u, :, :], ACT.Copy).then_inc(q_hi_made, 1)

            evac_xnT(0, 0)
            evac_q(0, 0)
            act.wait_ge(p_zeroed, 1)

            def exp(t, u, q):
                act.wait_ge(diff_made, 4 * t + q + 1)
                if q == 0 and (not isinstance(t, int) or t >= 2):
                    act.wait_ge(fold_made, 5 * (t - 1))
                    act.wait_ge(t_psum, 5 * (t - 1))
                act.activation(pm[u][:, 4 * q:4 * q + 4, :], diff[u][:, 4 * q:4 * q + 4, 0:P],
                               ACT.Exp).then_inc(p_made, 1)

            def evac_t(t, k, u):
                act.wait_ge(t_psum, 5 * t + k + 1)
                if not isinstance(t, int) or t >= 1:
                    act.wait_ge(pv_psum, t)
                act.activation(PT[:, k, :, :], ps_t[(5 * u + k) % 2][:, :].rearrange("p (a n) -> p a n", a=4),
                               ACT.Copy).then_inc(t_made, 1)

            def step(t, u, i, has):
                v = 1 - u
                if has(-1):
                    evac_t(t - 1, 2, v)
                if has(1):
                    evac_xnT(t + 1, v)
                if has(-1):
                    evac_t(t - 1, 3, v)
                if has(0):
                    exp(t, u, 0)
                if has(-1):
                    evac_t(t - 1, 4, v)
                if has(1):
                    evac_q(t + 1, v)
                if has(0):
                    exp(t, u, 1)
                if has(-2):
                    act.wait_ge(xn2T_psum, t - 1)
                    if not isinstance(t, int) or t >= 3:
                        act.wait_ge(lg_psum, t - 2)
                    act.activation(xn2T[:, :, :], ps_c[:, 0:KC * P].rearrange("p (c n) -> p c n", c=KC),
                                   ACT.Copy).then_inc(xn2T_made, 1)
                if has(0):
                    exp(t, u, 2)
                if has(-1):
                    act.wait_ge(rT_psum, t)
                    if not isinstance(t, int) or t >= 2:
                        act.wait_ge(OT_made, t - 1)
                    act.activation(rT[:, :, :], ps_a[:, D:2 * D].rearrange("p (g n) -> p g n", g=GROUPS),
                                   ACT.Copy).then_inc(rT_made, 1)
                if has(0):
                    evac_t(t, 0, u)
                    evac_t(t, 1, u)
                    exp(t, u, 3)
                    act.activation(pr[:, u, :, 0:REM], diff[u][:, :, P:KEYS], ACT.Exp).then_inc(pr_made, 1)
            steps(act, step)

            act.wait_ge(r_shift, 1)
            act.activation(r_ex[:, :, :], r_a[:, :, :], ACT.Exp).then_inc(r_exp, 1)
            act.wait_ge(r_shift, 2)
            act.activation(r_e2[:, :], r_s[:, :], ACT.Exp).then_inc(r_exp, 1)

            def split_weights(e, par, n):
                act.wait_ge(w_loaded, 16 * e + 16)
                dst = WS[:, par, 0, n * WH:(n + 1) * WH] if isinstance(par, int) else \
                    WS[:, bass.ds(par, 1), 0, n * WH:(n + 1) * WH].squeeze(1)
                act.activation(dst, wraw[:, n * WH:(n + 1) * WH], ACT.Copy).then_inc(w_hi, 1)
            for n in range(HALVES):
                split_weights(0, 0, n)

            act.wait_ge(at_slot_made, 1)
            act.activation(coded[:, :, 0, :], at_slot[:, :, :], ACT.Copy, scale=lane_sb[:, 0:1]).then_inc(coded_made, 1)

            def gelu(s):
                act.wait_ge(up_psum, s + 1)
                if not isinstance(s, int) or s >= 1:
                    act.wait_ge(hidT_psum, s)
                act.activation(hid.rearrange("p (c n) -> p c n", c=2), ps_s[0][:, :, :],
                               ACT.Gelu).then_inc(hid_made, 1)

            act.activation(r_e2[:, 0:1], lane_sb[:, :], ACT.Gelu)
            act.wait_ge(tables_made, 1)
            read_used(act)
            gelu(0)

            def slot(s, u, i, has):
                if has(1):
                    to_split = act.value_load(table(t_split, s), min_val=0, max_val=4 * E - 1)
                act.wait_ge(hidT_psum, s + 1)
                if not isinstance(s, int) or s >= 1:
                    act.wait_ge(down_psum, s)
                for a in range(2):
                    act.activation(hidT[:, 0, 4 * a:4 * a + 4, :], ps_t[a][:, :].rearrange("p (a n) -> p a n", a=4),
                                   ACT.Copy).then_inc(hidT_hi, 1)
                if has(1):
                    with act.If(to_split > 0):
                        e = to_split % E
                        with act.If(to_split % (2 * E) >= E):
                            split_weights(e, e % 2, 0)
                        with act.If(to_split >= 2 * E):
                            split_weights(e, e % 2, 1)
                    with if_used(act, s + 1):
                        gelu(s + 1)
            ff_slots(act, slot)

        @block.vector
        def _(dve):
            dve.wait_ge(ld_x0, 32)

            def wait_alone(s, n):
                dve.wait_ge(s, n)
                if not isinstance(n, int):
                    dve.sem_inc(dve_passed, 1)

            def x_tile(t):
                return xs[:, t, :] if isinstance(t, int) else xs[:, bass.ds(t, 1), :].squeeze(1)

            def sums1(t, u):
                if not isinstance(t, int) or t >= 2:
                    dve.wait_ge(xn_made, t - 1)
                dve.bn_stats(st1[:, u, :], x_tile(t)).then_inc(st1_made, 1)

            def aggregate(t, u, st, st_made, mv, mv_made):
                wait_alone(st_made, t + 1)
                dve.bn_aggr(mv[:, u, 0:2], st[:, u, :]).then_inc(mv_made, 1)

            def add_eps(t, u, mv, mv_made, var_made):
                dve.wait_ge(mv_made, t + 1)
                dve.tensor_scalar(mv[:, u, 2:3], mv[:, u, 1:2], EPS, None, ALU.add).then_inc(var_made, 1)

            def norm1(t, u):
                dve.wait_ge(rstd1_made, t + 1)
                if not isinstance(t, int) or t >= 2:
                    dve.wait_ge(xnT_psum, t - 1)
                dve.tensor_scalar(xn[:, u, :], x_tile(t), mv1[:, u, 0:1], mv1[:, u, 3:4],
                                  ALU.subtract, ALU.mult).then_inc(xn_made, 1)

            def norm2(t, u, i):
                dve.wait_ge(rstd2_made, t + 1)
                if not isinstance(t, int) or t >= 2:
                    dve.wait_ge(xr_stored[u], 16 * i)
                    dve.wait_ge(xn2T_psum, t - 1)
                dve.tensor_scalar(xn2[:, u, :], x1[:, u, :], mv2[:, u, 0:1], mv2[:, u, 3:4],
                                  ALU.subtract, ALU.mult).then_inc(xn2_made, 1)
            for t in range(2):
                sums1(t, t)
                aggregate(t, t, st1, st1_made, mv1, mv1_made)
                add_eps(t, t, mv1, mv1_made, var1_made)
            norm1(0, 0)
            norm1(1, 1)

            dve.wait_ge(ld_k, 64)
            dve.wait_ge(k_psum, 1)
            for g in range(GROUPS):
                dve.tensor_scalar(KT[:, g, :], ps_s[0][:, g, 0:B * KEYS], bk_sb[:, g:g + 1], None,
                                  ALU.add).then_inc(k_made, 1)
            dve.wait_ge(k_made, 2)
            dve.tensor_copy(KTr[:, 0, :, :], KT).then_inc(kt_hi, 1)
            dve.wait_ge(kt_hi, 1)
            dve.tensor_tensor(KTr[:, 1, :, :], KT, KTr[:, 0, :, :].bitcast(fp32), ALU.subtract).then_inc(kt_lo, 1)
            dve.wait_ge(kt_lo, 1)
            block_keys(dve, 0, 0, kb_made)
            dve.wait_ge(ld_v, 32)
            dve.wait_ge(v_psum, 1)
            dve.wait_ge(v_zeroed, 1)
            for b in range(B):
                vm = V_all[:, b, 0:HEADS * 32].rearrange("p (r a c) -> p r a c", a=2, c=32)
                vr = V_all[:, b, HEADS * 32:VW].rearrange("p (q c) -> p q c", c=64)
                main = ps_s[1][:, b, 0:D].rearrange("p (r a c) -> p r a c", a=2, c=DK)
                bvm = bv_sb[:, :].rearrange("p (r a c) -> p r a c", a=2, c=DK)
                for a in range(2):
                    dve.tensor_tensor(vm[:, :, a, DK * a:DK * a + DK], main[:, :, a, :], bvm[:, :, a, :],
                                      ALU.add).then_inc(v_made, 1)
                for j in range(4):
                    lanes = slice(32 * j, 32 * j + REM)
                    rest = ps_s[1][lanes, b, D:2 * D].rearrange("p (q j c) -> p q j c", j=4, c=DK)
                    bvr = bv_sb[lanes, :].rearrange("p (q j c) -> p q j c", j=4, c=DK)
                    dve.tensor_tensor(vr[lanes, :, DK * j:DK * j + DK], rest[:, :, j, :], bvr[:, :, j, :],
                                      ALU.add).then_inc(v_made, 1)

            dve.wait_ge(ld_x1, 16)
            dve.wait_ge(kb_made, 2)

            def split_heads(q):
                return ps_s[q % 2][:, :, 0:2 * KEYS].rearrange("p b (h k) -> p b h k", h=2), \
                    mx[:, q % 2, :].rearrange("p (b h) -> p b h", b=2)

            def maxima(t, q):
                dve.wait_ge(s_psum, 4 * t + q + 1)
                src, m = split_heads(q)
                dve.tensor_reduce(m, src, AX.X, ALU.max).then_inc(mx_made, 1)

            def shift(t, u, q):
                dve.wait_ge(mx_made, 4 * t + q + 1)
                if q == 0 and (not isinstance(t, int) or t >= 2):
                    dve.wait_ge(pr_made, t - 1)
                src, m = split_heads(q)
                dst = diff[u][:, 4 * q:4 * q + 4, :].rearrange("p (b h) k -> p b h k", b=2)
                dve.tensor_tensor(dst, src, m.unsqueeze(3).to_broadcast([P, 2, 2, KEYS]),
                                  ALU.subtract).then_inc(diff_made, 1)

            def step(t, u, i, has):
                v = 1 - u
                if has(0):
                    maxima(t, 0)
                if has(0):
                    shift(t, u, 0)
                if has(-2):
                    dve.wait_ge(wo_psum, t - 1)
                    dve.wait_ge(xb_made, t - 1)
                    if not isinstance(t, int) or t >= 4:
                        dve.wait_ge(x1_stored[u], 16 * (i - 1))
                        dve.wait_ge(xn2_made, t - 3)
                    dve.tensor_tensor(x1[:, u, :], ps_c[:, 0:D], xb[:, u, :], ALU.add).then_inc(x1_made, 1)
                if has(0):
                    maxima(t, 1)
                if has(-2):
                    dve.wait_ge(x1_made, t - 1)
                    dve.bn_stats(st2[:, u, :], x1[:, u, :]).then_inc(st2_made, 1)
                if has(0):
                    shift(t, u, 1)
                if has(-2):
                    aggregate(t - 2, u, st2, st2_made, mv2, mv2_made)
                if has(2):
                    sums1(t + 2, u)
                if has(-2):
                    add_eps(t - 2, u, mv2, mv2_made, var2_made)
                if has(0):
                    maxima(t, 2)
                if has(-2):
                    norm2(t - 2, u, i - 1)
                if has(2):
                    aggregate(t + 2, u, st1, st1_made, mv1, mv1_made)
                if has(0):
                    shift(t, u, 2)
                if has(-1):
                    dve.wait_ge(fold_made, 5 * t)
                    dve.tensor_reduce(den[:, :], fold[:, v, :, :], AX.X, ALU.add).then_inc(den_made, 1)
                if has(2):
                    add_eps(t + 2, u, mv1, mv1_made, var1_made)
                if has(-1):
                    dve.wait_ge(den_made, t)
                    dve.reciprocal(rec[:, :], den[:, :]).then_inc(rec_made, 1)
                    dve.wait_ge(rec_made, t)
                    if not isinstance(t, int) or t >= 2:
                        dve.wait_ge(rT_psum, t - 1)
                    dve.tensor_copy(rden[:, :, :], rec[:, :].unsqueeze(2).to_broadcast([P, HEADS, DK]))\
                       .then_inc(rden_made, 1)
                if has(0):
                    maxima(t, 3)
                if has(2):
                    norm1(t + 2, u)
                if has(0):
                    shift(t, u, 3)
                if has(-1):
                    dve.wait_ge(rT_made, t)
                    if not isinstance(t, int) or t >= 3:
                        dve.wait_ge(wo_psum, t - 2)
                    dve.tensor_tensor(OT[:, v, :, :], ps_a[:, 0:D].rearrange("p (g n) -> p g n", g=GROUPS),
                                      rT[:, :, :], ALU.mult).then_inc(OT_made, 1)
                if has(-2):
                    dve.wait_ge(lg_psum, t - 1)
                    lt = LG[:, t - 2, :] if isinstance(t, int) else LG[:, bass.ds(t - 2, 1), :].squeeze(1)
                    dve.tensor_copy(lt, ps_c[:, 0:E]).then_inc(lg_made, 1)
            steps(dve, step)

            done = [0]

            def then(ins):
                done[0] += 1
                ins.then_inc(r_step, 1)
                dve.wait_ge(r_step, done[0])

            wide = [P, TILES, E]
            bc_t = lambda a: a.unsqueeze(2).to_broadcast(wide)
            bc_e = lambda a: a.unsqueeze(1).to_broadcast(wide)
            dve.wait_ge(lg_made, TILES)
            dve.wait_ge(ld_c, 80)
            then(dve.tensor_copy(before_bf[:, :], before_sb[:, :]))

            def top(src, m, o):
                then(dve.tensor_reduce(m, src, AX.X, ALU.max))
                then(dve.tensor_tensor(r_b[:, :, :], src, bc_t(m), ALU.is_ge))
                then(dve.tensor_tensor(r_b[:, :, :], r_b[:, :, :], bc_e(em8_sb[:, :]), ALU.mult))
                then(dve.tensor_reduce(r_c[:, :], r_b[:, :, :], AX.X, ALU.min))
                then(dve.tensor_tensor(o, bc_e(em8_sb[:, :]), bc_t(r_c[:, :]), ALU.is_equal))

            def first_tables():
                wide = [1, SLOTS + 1, E]
                then(dve.tensor_tensor(t_cmp[:, :, :], count_sb[0:1, 0:SLOTS + 1].unsqueeze(2).to_broadcast(wide),
                                       r_st[0:1, :].unsqueeze(1).to_broadcast(wide), ALU.is_ge))
                then(dve.tensor_reduce(t_e[:, :], t_cmp[:, :, :], AX.X, ALU.add))
                then(dve.scalar_tensor_tensor(t_sum[:, :], t_e[:, 1:SLOTS + 1], float(E), t_e[:, 0:SLOTS],
                                              ALU.mult, ALU.add))
                then(dve.tensor_scalar(t_pair[:, :], t_sum[:, :], -float(E + 1), None, ALU.add))

            top(LG[:, :, :], r_m1[:, :], r_o1[:, :, :])
            dve.tensor_tensor(r_a[:, :, :], LG[:, :, :], bc_t(r_m1[:, :]), ALU.subtract).then_inc(r_shift, 1)
            then(dve.scalar_tensor_tensor(r_rank[:, 0:TILES, :], r_o1[:, :, :], -3e38, LG[:, :, :], ALU.mult, ALU.add))
            top(r_rank[:, 0:TILES, :], r_m2[:, :], r_o2[:, :, :])
            dve.tensor_tensor(r_s[:, :], r_m2[:, :], r_m1[:, :], ALU.subtract).then_inc(r_shift, 1)
            then(dve.memset(r_pick[:, TILES, :], 0.0))
            dve.tensor_tensor(r_pick[:, 0:TILES, :], r_o1[:, :, :], r_o2[:, :, :], ALU.add).then_inc(pick_made, 1)
            dve.wait_ge(r_exp, 2)
            then(dve.tensor_reduce(r_c[:, :], r_ex[:, :, :], AX.X, ALU.add))
            then(dve.reciprocal(wts[:, :, 0], r_c[:, :]))
            dve.tensor_tensor(wts[:, :, 1], r_e2[:, :], wts[:, :, 0], ALU.mult).then_inc(wts_made, 1)
            dve.wait_ge(rank_psum, 1)
            then(dve.tensor_copy(r_rank[:, :, :], ps_a[:, 0:(TILES + 1) * E].rearrange("p (t e) -> p t e", e=E)))
            then(dve.tensor_scalar(r_i[:, :], r_rank[:, TILES, :], float(P - 1), None, ALU.add))
            then(dve.tensor_scalar(r_i2[:, :], r_i[:, :], 7, None, ALU.logical_shift_right))
            then(dve.tensor_scalar(r_n[:, :], r_i2[:, :], 1.0, None, ALU.max))
            then(dve.memset(r_p[:, :, :], 0.0))
            then(dve.tensor_copy(r_p[:, 0, 4:4 + E], r_n[:, :]))
            for n, d in enumerate((1, 2, 4)):
                then(dve.tensor_tensor(r_p[:, 1 - n % 2, 4:4 + E], r_p[:, n % 2, 4:4 + E],
                                       r_p[:, n % 2, 4 - d:4 + E - d], ALU.add))
            then(dve.tensor_tensor(r_st[:, :], r_p[:, 1, 4:4 + E], r_n[:, :], ALU.subtract))
            then(dve.tensor_scalar(r_base[:, :], r_st[:, :], float(P), None, ALU.mult))
            then(dve.tensor_tensor(r_a[:, :, :], r_rank[:, 0:TILES, :], bc_e(r_base[:, :]), ALU.add))
            for k, o in ((0, r_o1), (1, r_o2)):
                then(dve.tensor_tensor(r_b[:, :, :], r_a[:, :, :], o[:, :, :], ALU.mult))
                then(dve.tensor_reduce(r_pos[:, k, :], r_b[:, :, :], AX.X, ALU.add))
            then(dve.tensor_copy(pos_i[:, :], r_pos[:, :, :].rearrange("p k t -> p (k t)")))
            then(dve.tensor_scalar(slot_i[:, :], pos_i[:, :], 7, None, ALU.logical_shift_right))
            then(dve.tensor_scalar(slot_f[:, :], slot_i[:, :], 0.0, None, ALU.max))
            dve.tensor_tensor(at_slot[:, :, :], count_sb[:, 0:SLOTS].unsqueeze(1).to_broadcast([P, PICKS, SLOTS]),
                              slot_f[:, :].unsqueeze(2).to_broadcast([P, PICKS, SLOTS]),
                              ALU.is_equal).then_inc(at_slot_made, 1)
            then(dve.scalar_tensor_tensor(lane_f[:, :], slot_f[:, :], -float(P),
                                          r_pos[:, :, :].rearrange("p k t -> p (k t)"), ALU.mult, ALU.add))
            for k in range(4):
                picks = slice(8 * k, 8 * k + 8)
                dve.tensor_tensor(at_lane[:, picks, :], count_sb[:, :].unsqueeze(1).to_broadcast([P, 8, P]),
                                  lane_f[:, picks].unsqueeze(2).to_broadcast([P, 8, P]),
                                  ALU.is_equal).then_inc(at_lane_made, 1)
            first_tables()

            def split_weights(e, par, n):
                dve.wait_ge(w_hi, HALVES * e + n + 1)
                at = (slice(None), par) if isinstance(par, int) else (slice(None), bass.ds(par, 1))
                hi, lo = (WS[at + (k, slice(n * WH, (n + 1) * WH))] for k in range(2))
                if not isinstance(par, int):
                    hi, lo = hi.squeeze(1), lo.squeeze(1)
                dve.tensor_tensor(lo, wraw[:, n * WH:(n + 1) * WH], hi.bitcast(fp32),
                                  ALU.subtract).then_inc(w_lo, 1)
            dve.wait_ge(codes_psum, 1)
            then(dve.tensor_copy(codes[:, :, :], ps_c[:, 0:2 * SLOTS].rearrange("p (v s) -> p v s", v=2)))
            src, code = codes[:, 0, :], codes[:, 1, :]
            then(dve.tensor_scalar(t_k[:, 1, :], code, -1.5 * TILES, None, ALU.is_lt))
            then(dve.tensor_scalar(t_k[:, 0, :], t_k[:, 1, :], -1.0, 1.0, ALU.mult, ALU.add))
            then(dve.scalar_tensor_tensor(t_a[:, :], code, float(P), src, ALU.mult, ALU.add))
            then(dve.scalar_tensor_tensor(t_a[:, :], t_k[:, 1, :], float(2 * TILES * P), t_a[:, :], ALU.mult, ALU.add))
            then(dve.tensor_scalar(t_b[:, :], code, -0.5, None, ALU.is_ge))
            then(dve.tensor_scalar(t_b[:, :], t_b[:, :], lane_sb[:, 0:1], float(TOK), ALU.mult, ALU.add))
            dve.tensor_tensor(tok_i[:, :], t_a[:, :], t_b[:, :], ALU.add).then_inc(toks_made, 1)
            dve.wait_ge(toks_made, 1)
            dve.tensor_copy(gtok[:, :], tok_i[:, 0:4]).then_inc(gtok_made, 1)

            then(dve.tensor_copy(t_used[:, :], r_p[0:1, 1, 3 + E:4 + E]))
            then(dve.scalar_tensor_tensor(t_val[:, :], t_e[:, 0:SLOTS], float(E) - 0.5, t_e[:, 0:SLOTS],
                                          ALU.is_lt, ALU.mult))
            then(dve.memset(t_first[:, :], 0.0))
            then(dve.memset(t_first[:, 1:2], 1.0))
            then(dve.tensor_tensor(t_first[:, 2:SLOTS + 1], t_e[:, 1:SLOTS], t_e[:, 0:SLOTS - 1], ALU.subtract))
            then(dve.tensor_tensor(t_short[:, :], t_first[:, 1:SLOTS + 2], t_first[:, 2:SLOTS + 3], ALU.max))
            then(dve.tensor_tensor(t_short[:, :], t_short[:, :], t_first[:, 0:SLOTS + 1], ALU.mult))
            then(dve.tensor_tensor(t_tmp[:, :], t_short[:, 1:SLOTS + 1], t_short[:, 0:SLOTS], ALU.subtract))
            then(dve.tensor_tensor(t_tmp[:, :], t_tmp[:, :], t_first[:, 0:SLOTS], ALU.add))
            then(dve.scalar_tensor_tensor(t_sum[:, :], t_tmp[:, :], 2.0, t_first[:, 1:SLOTS + 1], ALU.mult, ALU.add))
            then(dve.tensor_scalar(t_short[:, 0:SLOTS], t_e[:, 0:SLOTS], float(E) - 0.5, None, ALU.is_lt))
            then(dve.tensor_tensor(t_sum[:, :], t_sum[:, :], t_short[:, 0:SLOTS], ALU.mult))
            then(dve.tensor_tensor(t_tmp[:, :], t_tmp[:, :], t_first[:, 1:SLOTS + 1], ALU.max))
            then(dve.tensor_tensor(t_tmp[:, :], t_tmp[:, :], t_val[:, :], ALU.mult))
            dve.scalar_tensor_tensor(t_split[:, :], t_sum[:, :], float(E), t_tmp[:, :],
                                     ALU.mult, ALU.add).then_inc(tables_made, 1)

            def column(a, s):
                return a[:, s:s + 1] if isinstance(s, int) else a[:, bass.ds(s, 1)]

            def take_rows(s, u, more):
                dve.wait_ge(xgT_psum, s + 1)
                if not isinstance(s, int) or s >= 2:
                    dve.wait_ge(up_psum, s - 1)
                turned = ps_c[:, 0:D].rearrange("p (c n) -> p c n", c=KC)
                dve.tensor_copy(xgT[:, u % 2, 0, :, :], turned).then_inc(xgT_hi, 1)
                if more:
                    dve.tensor_copy(gtok[:, u:u + 1], column(tok_i, s + 4)).then_inc(gtok_made, 1)
                dve.wait_ge(xgT_hi, s + 1)
                dve.tensor_tensor(xgT[:, u % 2, 1, :, :], turned, xgT[:, u % 2, 0, :, :].bitcast(fp32),
                                  ALU.subtract).then_inc(xgT_made, 1)
                if not isinstance(s, int) or s >= 4:
                    dve.wait_ge(added, 16 * (s - 3))
                dve.tensor_tensor(wrow[:, u, 0:2], XG[:, u, D:D + 2],
                                  t_k[:, :, s] if isinstance(s, int) else t_k[:, :, bass.ds(s, 1)].squeeze(2),
                                  ALU.mult).then_inc(wr1, 1)
                dve.tensor_copy(rowtok[:, u:u + 1], column(tok_i, s))
                dve.wait_ge(wr1, s + 1)
                dve.tensor_tensor(wrow[:, u, 3:4], wrow[:, u, 0:1], wrow[:, u, 1:2], ALU.add).then_inc(wrow_made, 1)
            take_rows(0, 0, True)
            take_rows(1, 1, True)

            def slot(s, u, i, has):
                if has(1):
                    to_split = dve.value_load(table(t_split, s), min_val=0, max_val=4 * E - 1)
                for a in range(2):
                    dve.wait_ge(hidT_hi, 2 * s + a + 1)
                    dve.tensor_tensor(hidT[:, 1, 4 * a:4 * a + 4, :], ps_t[a][:, :].rearrange("p (a n) -> p a n", a=4),
                                      hidT[:, 0, 4 * a:4 * a + 4, :].bitcast(fp32), ALU.subtract).then_inc(hidT_lo, 1)
                if has(2):
                    take_rows(s + 2, (u + 2) % 4, has(6))
                if has(1):
                    with dve.If(to_split > 0):
                        e = to_split % E
                        with dve.If(to_split % (2 * E) >= E):
                            split_weights(e, e % 2, 0)
                        with dve.If(to_split >= 2 * E):
                            split_weights(e, e % 2, 1)
                dve.wait_ge(down_psum, s + 1)
                dve.wait_ge(wrow_made, s + 1)
                if not isinstance(s, int) or s >= 2:
                    dve.wait_ge(added, 16 * (s - 1))
                dve.tensor_scalar(ys[:, u % 2, :], ps_s[1][:, u % 2, 0:D], wrow[:, u, 3:4], None,
                                  ALU.mult).then_inc(ys_made, 1)
            dve.wait_ge(tables_made, 1)
            dve.wait_ge(tables_made, 1)
            read_used(dve)
            ff_slots(dve, slot)

        @block.tensor
        def _(pe):
            mm = pe.matmul

            def keep_busy(n):
                for _ in range(n):
                    mm(ps_t[0][:, :].rearrange("p (a n) -> p a n", a=4), ones_bf[:, :],
                       ones_bf[:, :].unsqueeze(1).to_broadcast([P, 4, P]), start=True, stop=True)
            pe.wait_ge(const_made, 2)
            keep_busy(12)
            pe.wait_ge(ld_k, 64)
            for g in range(GROUPS):
                for c in range(KC):
                    last = mm(ps_s[0][:, g, 0:B * KEYS], wk_sb[:, c, g * P:(g + 1) * P], ctx_sb[:, c, :],
                              start=c == 0, stop=c == KC - 1)
            last.then_inc(k_psum, 1)
            def xn_transposes(t, u):
                pe.wait_ge(xn_made, t + 1)
                if not isinstance(t, int) or t >= 3:
                    pe.wait_ge(OT_made, t - 2)
                for c in range(KC):
                    last = pe.transpose(ps_a[:, c * P:(c + 1) * P], xn[:, u, c * P:(c + 1) * P], id_sb[:, :])
                last.then_inc(xnT_psum, 1)

            def q_product(t, u):
                pe.wait_ge(xnT_made, t + 1)
                for g in range(GROUPS):
                    for c in range(KC):
                        last = mm(ps_a[:, D + g * P:D + (g + 1) * P], wq_sb[:, c, g * P:(g + 1) * P],
                                  xnT[:, u, c, :], start=c == 0, stop=c == KC - 1)
                last.then_inc(q_psum, 1)

            pe.wait_ge(ld_q, 48)
            xn_transposes(0, 0)
            pe.wait_ge(ld_v, 32)
            for b in range(B):
                for c in range(KC):
                    mm(ps_s[1][:, b, 0:D], ctx_sb[:, c, b * KEYS:b * KEYS + P], wv_sb[:, c, :],
                       start=c == 0, stop=c == KC - 1)
                for c in range(KC):
                    for j in range(4):
                        last = mm(ps_s[1][32 * j:32 * j + REM, b, D:2 * D],
                                  ctx_sb[:, c, b * KEYS + P:(b + 1) * KEYS], wv_sb[:, c, :],
                                  start=c == 0, stop=c == KC - 1)
            last.then_inc(v_psum, 1)
            q_product(0, 0)

            def scores(t, u, q):
                n = 4 * t + q
                if q == 0:
                    pe.wait_ge(q_split, t + 1)
                if q >= 2 or not isinstance(t, int) or t >= 1:
                    pe.wait_ge(diff_made, n - 1)
                g, j0 = q // 2, 4 * (q % 2)
                if g == 1 and isinstance(t, int) and t == 0:
                    pe.wait_ge(kg1_made, 2)
                for j in range(2):
                    for k, (a, kb) in enumerate(((q_hi, kb_hi), (q_hi, kb_lo), (q_lo, kb_hi))):
                        if isinstance(t, int):
                            rhs = kb[:, t // (TILES // B), g, j0 + 2 * j:j0 + 2 * j + 2, :]
                        else:
                            rhs = kb[:, bass.ds(t // (TILES // B), 1), g, j0 + 2 * j:j0 + 2 * j + 2, :].squeeze(1)
                        last = mm(ps_s[q % 2][:, j, 0:2 * KEYS].rearrange("p (h k) -> p h k", h=2),
                                  a[:, u, g, :], rhs, start=k == 0, stop=k == 2)
                last.then_inc(s_psum, 1)

            def p_transposes(t, k, u):
                if not isinstance(t, int) or 5 * t + k >= 2:
                    pe.wait_ge(t_made, 5 * t + k - 1)
                if k < 4:
                    pe.wait_ge(p_made, 4 * t + k + 1)
                else:
                    pe.wait_ge(pr_made, t + 1)
                for j in range(4):
                    src = pm[u][:, 4 * k + j, :] if k < 4 else \
                        pr[:, u, 4 * j:4 * j + 4, :].rearrange("p h k -> p (h k)")
                    last = pe.transpose(ps_t[(5 * u + k) % 2][:, j * P:(j + 1) * P], src, id_sb[:, :])
                last.then_inc(t_psum, 1)

            def pv(t, u, i):
                pe.wait_ge(t_made, 5 * t + 5)
                pe.wait_ge(vcur_made[u], 16 * i + 16)
                if not isinstance(t, int) or t < TILES - 2:
                    pe.wait_ge(qf_made, t + 3)
                for g in range(GROUPS):
                    cols = slice(g * P, (g + 1) * P)
                    for a in range(2):
                        qd = 2 * g + a
                        mm(ps_a[64 * a:64 * a + 64, cols], V_cur[:, u, HEADS * 32 + 64 * qd:HEADS * 32 + 64 * qd + 64],
                           PT[:, 4, qd, :], start=True, stop=True, skip_group_check=True)
                    for a in range(2):
                        for r in range(4):
                            h = g * GH + 2 * r + a
                            last = mm(ps_a[32 * r:32 * r + 32, cols], V_cur[:, u, 32 * h:32 * h + 32],
                                      PT[:, h // 4, h % 4, :], start=False, stop=True, skip_group_check=True)
                last.then_inc(pv_psum, 1)

            def rec_transposes(t):
                pe.wait_ge(rden_made, t + 1)
                for g in range(GROUPS):
                    last = pe.transpose(ps_a[:, D + g * P:D + (g + 1) * P],
                                        rden[:, g * GH:(g + 1) * GH, :].rearrange("p h c -> p (h c)"), id_sb[:, :])
                last.then_inc(rT_psum, 1)

            def wo_product(t, u):
                pe.wait_ge(OT_made, t + 1)
                if not isinstance(t, int) or t >= 1:
                    pe.wait_ge(lg_made, t)
                for g in range(GROUPS):
                    last = mm(ps_c[:, 0:D], OT[:, u, g, :], wo_sb[:, g, :], start=g == 0, stop=g == GROUPS - 1)
                last.then_inc(wo_psum, 1)

            def xn2_transposes(t, u):
                pe.wait_ge(xn2_made, t + 1)
                for c in range(KC):
                    last = pe.transpose(ps_c[:, c * P:(c + 1) * P], xn2[:, u, c * P:(c + 1) * P], id_sb[:, :])
                last.then_inc(xn2T_psum, 1)

            def router(t, u):
                pe.wait_ge(xn2T_made, t + 1)
                for c in range(KC):
                    last = mm(ps_c[:, 0:E], xn2T[:, c, :], rw_sb[:, c, :], start=c == 0, stop=c == KC - 1)
                last.then_inc(lg_psum, 1)

            def step(t, u, i, has):
                v = 1 - u
                if isinstance(t, int) and t == LOOP0 - 1:
                    pe.wait_ge(kb1_made, GROUPS * 2)
                if has(0):
                    scores(t, u, 1)
                if has(-2):
                    wo_product(t - 2, u)
                if has(-1):
                    p_transposes(t - 1, 2, v)
                if has(1):
                    xn_transposes(t + 1, v)
                if has(-1):
                    p_transposes(t - 1, 3, v)
                if has(0):
                    scores(t, u, 2)
                if has(-1):
                    p_transposes(t - 1, 4, v)
                if has(1):
                    q_product(t + 1, v)
                if has(0):
                    scores(t, u, 3)
                if has(-1):
                    pv(t - 1, v, i if v == 0 else i - 1)
                if has(-2):
                    xn2_transposes(t - 2, u)
                if has(1):
                    scores(t + 1, v, 0)
                if has(-1):
                    rec_transposes(t - 1)
                if has(0):
                    p_transposes(t, 0, u)
                if has(-2):
                    router(t - 2, u)
                if has(0):
                    p_transposes(t, 1, u)
            pe.wait_ge(kb_made, 2)
            scores(0, 0, 0)
            pe.wait_ge(v_made, B * 6)
            pe.wait_ge(ld_w, 48)
            steps(pe, step)

            pe.wait_ge(pick_made, 1)
            pe.wait_ge(const_made, 2)
            cols = ps_a[:, 0:(TILES + 1) * E].rearrange("p (t e) -> p t e", e=E)
            mm(cols, before_bf[:, :], r_pick[:, :, :], start=True, stop=True)
            for t in range(TILES):
                last = mm(cols[:, t + 1:TILES + 1, :], ones_bf[:, :],
                          r_pick[:, t:t + 1, :].to_broadcast([P, TILES - t, E]),
                          start=False, stop=True, skip_group_check=True)
            last.then_inc(rank_psum, 1)

            pe.wait_ge(coded_made, 2)
            for n in range(PICKS):
                if n % 8 == 0:
                    pe.wait_ge(at_lane_made, n // 8 + 1)
                last = mm(ps_c[:, 0:2 * SLOTS], at_lane[:, n, :], coded[:, n, :, :].rearrange("p v s -> p (v s)"),
                          start=n == 0, stop=n == PICKS - 1)
            last.then_inc(codes_psum, 1)

            def row_transposes(s, u):
                count = s // 4 + 1
                pe.wait_ge(xg_loaded[u], 16 * count)
                if not isinstance(s, int) or s >= 1:
                    pe.wait_ge(xgT_made, s)
                for c in range(KC):
                    last = pe.transpose(ps_c[:, c * P:(c + 1) * P], XG[:, u, c * P:(c + 1) * P], id_sb[:, :])
                last.then_inc(xgT_psum, 1)

            w1 = WS[:, :, :, 0:KC * HID].rearrange("p e s (c h) -> p e s c h", c=KC)
            w2 = WS[:, :, :, KC * HID:WB].rearrange("p e s (j d) -> p e s j d", j=HJ)
            PARTS = ((0, 0), (0, 1), (1, 0))

            def up(s, u, e):
                par = e % 2
                pe.wait_ge(w_hi, HALVES * e + HALVES)
                pe.wait_ge(w_lo, HALVES * e + HALVES)
                pe.wait_ge(xgT_made, s + 1)
                if not isinstance(s, int) or s >= 1:
                    pe.wait_ge(hid_made, s)
                for c in range(2):
                    for k in range(KC):
                        for n, (a, w) in enumerate(PARTS):
                            last = mm(ps_s[0][:, c, :], xgT[:, u % 2, a, k, :],
                                      w1[:, bass.ds(par, 1), w, k, 512 * c:512 * (c + 1)].squeeze(1),
                                      start=k == 0 and n == 0, stop=k == KC - 1 and n == 2)
                last.then_inc(up_psum, 1)

            def down(s, u, e):
                par = e % 2
                pe.wait_ge(hidT_lo, 2 * s + 2)
                if not isinstance(s, int) or s >= 2:
                    pe.wait_ge(ys_made, s - 1)
                for j in range(HJ):
                    for n, (a, w) in enumerate(PARTS):
                        last = mm(ps_s[1][:, u % 2, 0:D], hidT[:, a, j, :],
                                  w2[:, bass.ds(par, 1), w, j, :].squeeze(1),
                                  start=j == 0 and n == 0, stop=j == HJ - 1 and n == 2)
                last.then_inc(down_psum, 1)

            keep_busy(20)
            pe.wait_ge(toks_made, 1)
            row_transposes(0, 0)
            row_transposes(1, 1)
            pe.wait_ge(tables_made, 1)
            read_used(pe)
            up(0, 0, 0)

            def slot(s, u, i, has):
                pair = pe.value_load(table(t_pair, s), min_val=0, max_val=E * E - 1)
                e0, e1 = pair % E, pair // E
                pe.wait_ge(hid_made, s + 1)
                for j in range(HJ):
                    last = pe.transpose(ps_t[j // 4][:, (j % 4) * P:(j % 4 + 1) * P], hid[:, j * P:(j + 1) * P],
                                        id_sb[:, :])
                last.then_inc(hidT_psum, 1)
                if has(2):
                    row_transposes(s + 2, (u + 2) % 4)
                if has(1):
                    with if_used(pe, s + 1):
                        up(s + 1, (u + 1) % 4, e1)
                down(s, u, e0)
            ff_slots(pe, slot)


def kernel(x, ctx_1024, L0_xattn_Wq, L0_xattn_bq, L0_xattn_Wk, L0_xattn_bk, L0_xattn_Wv, L0_xattn_bv,
           L0_xattn_Wo, L0_xattn_bo, L0_ffn_router_w, L0_ffn_w1, L0_ffn_w2):
    import concourse.bacc as _bacc
    from concourse.bass_utils import run_bass_kernel_spmd as _run

    def laid(a, *order):
        return np.ascontiguousarray(np.asarray(a).transpose(*order)) if order else np.asarray(a)

    w1 = laid(L0_ffn_w1, 0, 2, 1).reshape(E, KC, P, HID).transpose(0, 2, 1, 3).reshape(E, P, KC * HID)
    w2 = laid(L0_ffn_w2, 0, 2, 1).reshape(E, HJ, P, D).transpose(0, 2, 1, 3).reshape(E, P, HJ * D)
    lanes = np.arange(P)
    data = {
        "x": laid(x).reshape(TOK, D),
        "ctxT": laid(ctx_1024, 2, 0, 1).reshape(D, B * KEYS),
        "wq": laid(L0_xattn_Wq, 1, 0, 2).reshape(D, D),
        "bq": laid(L0_xattn_bq).reshape(D),
        "wk": laid(L0_xattn_Wk, 1, 0, 2).reshape(D, D),
        "bk": laid(L0_xattn_bk).reshape(D),
        "wv": laid(L0_xattn_Wv, 1, 0, 2).reshape(D, D),
        "bv": laid(L0_xattn_bv).reshape(D),
        "wo": laid(L0_xattn_Wo),
        "bo": laid(L0_xattn_bo),
        "rwT": laid(L0_ffn_router_w, 1, 0),
        "wexp": np.concatenate([w1, w2], axis=2),
        "ident": np.eye(P, dtype=np.float32),
        "headmask": (lanes[:, None] // DK == np.arange(GH)[None]).astype(np.float32),
        "before": (lanes[:, None] < lanes[None]).astype(np.float32),
        "em8": np.broadcast_to(np.arange(E) - float(E), (P, E)).astype(np.float32),
        "count": np.broadcast_to(np.arange(P), (P, P)).astype(np.float32),
        "tilecode": np.broadcast_to(np.arange(TILES)[None] - TILES * np.array([[1], [3]]), (P, 2, TILES))
                      .reshape(P, PICKS).astype(np.float32),
        "lane": lanes[:, None].astype(np.float32),
    }
    nc = _bacc.Bacc("TRN2", target_bir_lowering=False, num_devices=1)
    arrays, args = {}, []
    for name, a in data.items():
        arrays[f"in_{name}"] = np.ascontiguousarray(a)
        args.append(nc.dram_tensor(f"in_{name}", a.shape, mybir.dt.from_np(a.dtype), kind="ExternalInput").ap())
    args.append(nc.dram_tensor("result", [TOK + P, D], mybir.dt.float32, kind="ExternalOutput").ap())
    xattn_moe_kernel(nc, *args)
    r = _run(nc, [arrays], core_ids=[0])
    return r.results[0]["result"][0:TOK].reshape(B, S, D)
```
